# Optimizing a Trainium2 kernel written in Bass

```python
import numpy as np
import jax
import jax.numpy as jnp

def _softmax(x, axis=-1):
    return jax.nn.softmax(x, axis=axis)

def _gelu(x):
    return jax.nn.gelu(x, approximate=True)

def _silu(x):
    return jax.nn.silu(x)

def _sigmoid(x):
    return jax.nn.sigmoid(x)

def _layernorm(x, axis=-1, eps=1e-05):
    m = jnp.mean(x, axis=axis, keepdims=True)
    v = jnp.var(x, axis=axis, keepdims=True)
    return (x - m) / jnp.sqrt(v + eps)

def _scatter_add(tgt, idx, src, axis=0):
    return tgt.at[idx].add(src)

def _segment_sum(src, seg, n):
    return jax.ops.segment_sum(src, seg, n)
kernel_name = 'mk_dlrm_tower_d1_rec_r8_62ba59'

def setup_inputs(seed: int=0):
    np.random.seed(seed)
    _w = jnp.asarray

    def _rec_inputs():
        import jax
        import jax.numpy as jnp
        _tk = jax.random.key(seed)
        dense_ctx = jax.random.normal(jax.random.fold_in(_tk, 190), (512, 16), jnp.float32)
        ids = jnp.stack([jax.random.randint(jax.random.fold_in(_tk, 200 + f), (512,), 0, v, jnp.int32) for f, v in enumerate([1250, 125000, 125000, 1000, 1000, 12500, 12500, 1250, 12500, 12500, 12500, 12500, 12500, 125000, 12500, 1250, 125000, 12500, 1250, 1250, 1000, 125000, 125000, 12500, 1000, 1250, 1000, 12500, 1250, 1000, 1250, 12500])], axis=1)
        tbl_0 = 0.05 * jax.random.normal(jax.random.fold_in(_tk, 500 + 0), (1250, 16), jnp.float32)
        tbl_1 = 0.05 * jax.random.normal(jax.random.fold_in(_tk, 500 + 1), (125000, 16), jnp.float32)
        tbl_2 = 0.05 * jax.random.normal(jax.random.fold_in(_tk, 500 + 2), (125000, 16), jnp.float32)
        tbl_3 = 0.05 * jax.random.normal(jax.random.fold_in(_tk, 500 + 3), (1000, 16), jnp.float32)
        tbl_4 = 0.05 * jax.random.normal(jax.random.fold_in(_tk, 500 + 4), (1000, 16), jnp.float32)
        tbl_5 = 0.05 * jax.random.normal(jax.random.fold_in(_tk, 500 + 5), (12500, 16), jnp.float32)
        tbl_6 = 0.05 * jax.random.normal(jax.random.fold_in(_tk, 500 + 6), (12500, 16), jnp.float32)
        tbl_7 = 0.05 * jax.random.normal(jax.random.fold_in(_tk, 500 + 7), (1250, 16), jnp.float32)
        tbl_8 = 0.05 * jax.random.normal(jax.random.fold_in(_tk, 500 + 8), (12500, 16), jnp.float32)
        tbl_9 = 0.05 * jax.random.normal(jax.random.fold_in(_tk, 500 + 9), (12500, 16), jnp.float32)
        tbl_10 = 0.05 * jax.random.normal(jax.random.fold_in(_tk, 500 + 10), (12500, 16), jnp.float32)
        tbl_11 = 0.05 * jax.random.normal(jax.random.fold_in(_tk, 500 + 11), (12500, 16), jnp.float32)
        tbl_12 = 0.05 * jax.random.normal(jax.random.fold_in(_tk, 500 + 12), (12500, 16), jnp.float32)
        tbl_13 = 0.05 * jax.random.normal(jax.random.fold_in(_tk, 500 + 13), (125000, 16), jnp.float32)
        tbl_14 = 0.05 * jax.random.normal(jax.random.fold_in(_tk, 500 + 14), (12500, 16), jnp.float32)
        tbl_15 = 0.05 * jax.random.normal(jax.random.fold_in(_tk, 500 + 15), (1250, 16), jnp.float32)
        tbl_16 = 0.05 * jax.random.normal(jax.random.fold_in(_tk, 500 + 16), (125000, 16), jnp.float32)
        tbl_17 = 0.05 * jax.random.normal(jax.random.fold_in(_tk, 500 + 17), (12500, 16), jnp.float32)
        tbl_18 = 0.05 * jax.random.normal(jax.random.fold_in(_tk, 500 + 18), (1250, 16), jnp.float32)
        tbl_19 = 0.05 * jax.random.normal(jax.random.fold_in(_tk, 500 + 19), (1250, 16), jnp.float32)
        tbl_20 = 0.05 * jax.random.normal(jax.random.fold_in(_tk, 500 + 20), (1000, 16), jnp.float32)
        tbl_21 = 0.05 * jax.random.normal(jax.random.fold_in(_tk, 500 + 21), (125000, 16), jnp.float32)
        tbl_22 = 0.05 * jax.random.normal(jax.random.fold_in(_tk, 500 + 22), (125000, 16), jnp.float32)
        tbl_23 = 0.05 * jax.random.normal(jax.random.fold_in(_tk, 500 + 23), (12500, 16), jnp.float32)
        tbl_24 = 0.05 * jax.random.normal(jax.random.fold_in(_tk, 500 + 24), (1000, 16), jnp.float32)
        tbl_25 = 0.05 * jax.random.normal(jax.random.fold_in(_tk, 500 + 25), (1250, 16), jnp.float32)
        tbl_26 = 0.05 * jax.random.normal(jax.random.fold_in(_tk, 500 + 26), (1000, 16), jnp.float32)
        tbl_27 = 0.05 * jax.random.normal(jax.random.fold_in(_tk, 500 + 27), (12500, 16), jnp.float32)
        tbl_28 = 0.05 * jax.random.normal(jax.random.fold_in(_tk, 500 + 28), (1250, 16), jnp.float32)
        tbl_29 = 0.05 * jax.random.normal(jax.random.fold_in(_tk, 500 + 29), (1000, 16), jnp.float32)
        tbl_30 = 0.05 * jax.random.normal(jax.random.fold_in(_tk, 500 + 30), (1250, 16), jnp.float32)
        tbl_31 = 0.05 * jax.random.normal(jax.random.fold_in(_tk, 500 + 31), (12500, 16), jnp.float32)
        _rk = jax.random.fold_in(_tk, 7)
        W_top1 = 0.0693375 * jax.random.normal(jax.random.fold_in(_tk, 801), (208, 512), jnp.float32)
        W_top2 = 0.0441942 * jax.random.normal(jax.random.fold_in(_tk, 802), (512, 256), jnp.float32)
        W_top3 = 0.0625 * jax.random.normal(jax.random.fold_in(_tk, 803), (256, 1), jnp.float32)
        b_top1 = jnp.zeros((512,), jnp.float32)
        b_top2 = jnp.zeros((256,), jnp.float32)
        return (dense_ctx, ids, tbl_0, tbl_1, tbl_2, tbl_3, tbl_4, tbl_5, tbl_6, tbl_7, tbl_8, tbl_9, tbl_10, tbl_11, tbl_12, tbl_13, tbl_14, tbl_15, tbl_16, tbl_17, tbl_18, tbl_19, tbl_20, tbl_21, tbl_22, tbl_23, tbl_24, tbl_25, tbl_26, tbl_27, tbl_28, tbl_29, tbl_30, tbl_31, W_top1, b_top1, W_top2, b_top2, W_top3)
    dense_ctx, ids, tbl_0, tbl_1, tbl_2, tbl_3, tbl_4, tbl_5, tbl_6, tbl_7, tbl_8, tbl_9, tbl_10, tbl_11, tbl_12, tbl_13, tbl_14, tbl_15, tbl_16, tbl_17, tbl_18, tbl_19, tbl_20, tbl_21, tbl_22, tbl_23, tbl_24, tbl_25, tbl_26, tbl_27, tbl_28, tbl_29, tbl_30, tbl_31, W_top1, b_top1, W_top2, b_top2, W_top3 = _rec_inputs()

    def _L0_rec_setup():
        import jax, jax.numpy as jnp
        import numpy as np
        B, M, D = (2048, 32, 16)
        LAYERS = [64, 64, 64]
        key = jax.random.key(seed)
        ks = jax.random.split(key, 4)
        inp = {'embeddings': jax.random.normal(ks[0], (B, M, D), dtype=jnp.float32)}
        hk_1 = M
        for i, hk in enumerate(LAYERS):
            scale = (2.0 / (M * hk_1 + hk)) ** 0.5
            inp[f'W{i}'] = jax.random.normal(ks[i + 1], (M, hk_1, hk), dtype=jnp.float32) * scale
            hk_1 = hk
        return inp
    _L0_rec_all = _L0_rec_setup()
    _L0_rec_in = {k: v for k, v in _L0_rec_all.items() if k in ('W0', 'W1', 'W2')}
    del _L0_rec_all
    return {'dense_ctx': dense_ctx, 'ids': ids, 'tbl_0': tbl_0, 'tbl_1': tbl_1, 'tbl_2': tbl_2, 'tbl_3': tbl_3, 'tbl_4': tbl_4, 'tbl_5': tbl_5, 'tbl_6': tbl_6, 'tbl_7': tbl_7, 'tbl_8': tbl_8, 'tbl_9': tbl_9, 'tbl_10': tbl_10, 'tbl_11': tbl_11, 'tbl_12': tbl_12, 'tbl_13': tbl_13, 'tbl_14': tbl_14, 'tbl_15': tbl_15, 'tbl_16': tbl_16, 'tbl_17': tbl_17, 'tbl_18': tbl_18, 'tbl_19': tbl_19, 'tbl_20': tbl_20, 'tbl_21': tbl_21, 'tbl_22': tbl_22, 'tbl_23': tbl_23, 'tbl_24': tbl_24, 'tbl_25': tbl_25, 'tbl_26': tbl_26, 'tbl_27': tbl_27, 'tbl_28': tbl_28, 'tbl_29': tbl_29, 'tbl_30': tbl_30, 'tbl_31': tbl_31, 'W_top1': W_top1, 'b_top1': b_top1, 'W_top2': W_top2, 'b_top2': b_top2, 'W_top3': W_top3, 'L0_rec_W0': _L0_rec_in['W0'], 'L0_rec_W1': _L0_rec_in['W1'], 'L0_rec_W2': _L0_rec_in['W2']}

def reference(dense_ctx, ids, tbl_0, tbl_1, tbl_2, tbl_3, tbl_4, tbl_5, tbl_6, tbl_7, tbl_8, tbl_9, tbl_10, tbl_11, tbl_12, tbl_13, tbl_14, tbl_15, tbl_16, tbl_17, tbl_18, tbl_19, tbl_20, tbl_21, tbl_22, tbl_23, tbl_24, tbl_25, tbl_26, tbl_27, tbl_28, tbl_29, tbl_30, tbl_31, W_top1, b_top1, W_top2, b_top2, W_top3, L0_rec_W0, L0_rec_W1, L0_rec_W2):
    import jax
    import jax.numpy as jnp

    def _L0_rec_ref(embeddings, W0, W1, W2):
        import jax, jax.numpy as jnp
        import numpy as np
        B, M, D = (2048, 32, 16)
        LAYERS = [64, 64, 64]
        x0 = embeddings
        xk = x0
        outs = []
        for W in (W0, W1, W2):
            xk = jax.nn.relu(jnp.einsum('bmd,bhd,mhk->bkd', x0, xk, W))
            outs.append(jnp.sum(xk, axis=2))
        return jnp.concatenate(outs, axis=1)
    e = jnp.stack([tbl_0[ids[:, 0]], tbl_1[ids[:, 1]], tbl_2[ids[:, 2]], tbl_3[ids[:, 3]], tbl_4[ids[:, 4]], tbl_5[ids[:, 5]], tbl_6[ids[:, 6]], tbl_7[ids[:, 7]], tbl_8[ids[:, 8]], tbl_9[ids[:, 9]], tbl_10[ids[:, 10]], tbl_11[ids[:, 11]], tbl_12[ids[:, 12]], tbl_13[ids[:, 13]], tbl_14[ids[:, 14]], tbl_15[ids[:, 15]], tbl_16[ids[:, 16]], tbl_17[ids[:, 17]], tbl_18[ids[:, 18]], tbl_19[ids[:, 19]], tbl_20[ids[:, 20]], tbl_21[ids[:, 21]], tbl_22[ids[:, 22]], tbl_23[ids[:, 23]], tbl_24[ids[:, 24]], tbl_25[ids[:, 25]], tbl_26[ids[:, 26]], tbl_27[ids[:, 27]], tbl_28[ids[:, 28]], tbl_29[ids[:, 29]], tbl_30[ids[:, 30]], tbl_31[ids[:, 31]]], axis=1)
    z = _L0_rec_ref(e, L0_rec_W0, L0_rec_W1, L0_rec_W2)
    z = z.reshape(z.shape[0], -1)
    h = jnp.concatenate([z, dense_ctx], axis=1)
    h = jnp.maximum(h @ W_top1 + b_top1, 0.0)
    h = jnp.maximum(h @ W_top2 + b_top2, 0.0)
    y = h @ W_top3
    return y

_drawn_inputs = setup_inputs


def setup_inputs(seed=0):
    import zlib

    import numpy as np

    out = dict(_drawn_inputs(seed))
    spreads = {'b_top1': (0.0, 2.0), 'b_top2': (0.0, 0.8)}
    factors = {'tbl_0': 8.0,
     'tbl_1': 8.0,
     'tbl_2': 8.0,
     'tbl_3': 8.0,
     'tbl_4': 8.0,
     'tbl_5': 8.0,
     'tbl_6': 8.0,
     'tbl_7': 8.0,
     'tbl_8': 8.0,
     'tbl_9': 8.0,
     'tbl_10': 8.0,
     'tbl_11': 8.0,
     'tbl_12': 8.0,
     'tbl_13': 8.0,
     'tbl_14': 8.0,
     'tbl_15': 8.0,
     'tbl_16': 8.0,
     'tbl_17': 8.0,
     'tbl_18': 8.0,
     'tbl_19': 8.0,
     'tbl_20': 8.0,
     'tbl_21': 8.0,
     'tbl_22': 8.0,
     'tbl_23': 8.0,
     'tbl_24': 8.0,
     'tbl_25': 8.0,
     'tbl_26': 8.0,
     'tbl_27': 8.0,
     'tbl_28': 8.0,
     'tbl_29': 8.0,
     'tbl_30': 8.0,
     'tbl_31': 8.0,
     'L0_rec_W0': 3.641,
     'L0_rec_W1': 8.0,
     'L0_rec_W2': 8.0,
     'dense_ctx': 7.477}
    for name, (base, spread) in spreads.items():
        noise = np.random.default_rng([zlib.crc32(name.encode()), seed]).standard_normal(out[name].shape)
        drawn = base * np.exp(spread * noise) if base else spread * noise
        out[name] = jnp.asarray(drawn.astype(out[name].dtype))
    for name, factor in factors.items():
        out[name] = (out[name] * factor).astype(out[name].dtype)
    return out
```

```python
from contextlib import ExitStack

import numpy as np

import concourse.bass as bass
from concourse import mybir

F32 = mybir.dt.float32
BF16 = mybir.dt.bfloat16
I32 = mybir.dt.int32
ALU = mybir.AluOpType
ACT = mybir.ActivationFunctionType
AX_X = mybir.AxisListType.X

B, M, D, H = 512, 32, 16, 64
P = 128
NT = B // P
CH = 512
DC = CH // P
PAIR = 2 * CH
NPAIR = D * P // PAIR
OUT1, OUT2, NCTX = 512, 256, 16

T1 = 5
T2 = M * H // P
PARTS = 3

DMA_TILES = (3, 4, 5, 6, 7, 8, 9, 10, 11, 12, 13, 14, 15)
KEPT_TILES = tuple(t for t in range(T2) if t not in DMA_TILES)
ORDER2 = (3, 4, 5, 0, 6, 7, 8, 1, 9, 10, 11, 2, 12, 13, 14, 15)
ORDER3 = DMA_TILES + KEPT_TILES
POOL_TILES = {("L2", 0): (5, 8, 11), ("L3", 0): (5, 8, 11, 14, 0),
              ("L2", 1): (5, 8, 11), ("L3", 1): (5, 8, 11, 14, 0)}
DVE_SLOTS = 6
POOL_SLOTS = 4
BC_SLOTS = 3
GATHERS_FIRST = 16
TURN_AT, HI_AT, REST_AT, MID_AT, LO_AT, KEEP_AT = 3, 4, 7, 8, 9, 9
AHEAD = (13, 14, 15)
SUM3_AT = 4


def fill_order():
    order = []
    for j in range(2):
        order += [("bc", j, t) for t in ORDER2 if t in KEPT_TILES]
        order += [("rep", j + 1, 0)] + [("shift", j + 1, t) for t in range(T1)]
    return order + [("none", 2, 0)] * (-len(order) % BC_SLOTS)


FILLS = fill_order()
REAL_FILLS = [x for x in FILLS if x[0] != "none"]
FIRST_FILLS = 1 + T1
COPIES = [x for x in FILLS if x[0] in ("bc", "rep")]
PRODUCTS = [(layer, j, t) for j in range(2) for layer, order in (("L2", ORDER2), ("L3", ORDER3)) for t in order]
DVE_PRODUCTS = [x for x in PRODUCTS if x[2] not in POOL_TILES[x[:2]]]
POOL_PRODUCTS = [x for x in PRODUCTS if x[2] in POOL_TILES[x[:2]]]
assert len(AHEAD) == BC_SLOTS
assert len(DVE_PRODUCTS) % DVE_SLOTS == 0 and len(POOL_PRODUCTS) % POOL_SLOTS == 0
assert all(("L2", j, ORDER2[-1]) in DVE_PRODUCTS and ("L3", j, ORDER3[-1]) in DVE_PRODUCTS for j in range(2))
assert all(x in DVE_PRODUCTS for x in PRODUCTS if x[0] == "L2" and x[2] in KEPT_TILES)


def interaction_tower(nc, ids, tables, sel, ident, w0a, w0b, w1, w2, ctx_t,
                      wt1, bt1, wt2, bt2, wt3, x_dram, out):
    with ExitStack() as ctx:
        def sb(name, shape, dt=F32):
            return ctx.enter_context(nc.sbuf_tensor(name, shape, dt))

        def sem(name):
            return ctx.enter_context(nc.semaphore(name))

        idx = sb("idx", [P, M], I32)
        emb = sb("emb", [P, M, D])
        sel_sb = sb("sel_sb", [PARTS * M, sel.shape[1]], BF16)
        id_sb = sb("id_sb", [P, P])
        x_hi = sb("x_hi", [P, CH], BF16)
        x_mid = sb("x_mid", [P, CH], BF16)
        x_lo = sb("x_lo", [P, CH], BF16)
        x_rest = sb("x_rest", [P, CH])
        xp = sb("xp", [PARTS * M, 2, PAIR], BF16)
        x_rep = sb("x_rep", [P, PAIR])
        x_all = sb("x_all", [P, CH])
        x_bc = sb("x_bc", [P, T2, PAIR])
        xk1 = sb("xk1", [P, PAIR])
        xk2 = sb("xk2", [P, PAIR])
        z1 = sb("z1", [P, T1, PAIR])
        z = sb("z", [P, DVE_SLOTS, PAIR])
        zp = sb("zp", [P, POOL_SLOTS, PAIR])
        relu = sb("relu", [P, 2, CH])
        sums = sb("sums", [P, 2, 3, B])
        w0_sb = sb("w0_sb", [P, T1, H])
        w0b_sb = sb("w0b_sb", [P, T1 - 1, H])
        w1_sb = sb("w1_sb", [P, T2, H])
        w2_sb = sb("w2_sb", [P, T2, H])
        wt1a_sb = sb("wt1a_sb", [P, OUT1])
        wt1b_sb = sb("wt1b_sb", [H + NCTX, OUT1])
        wt2_sb = sb("wt2_sb", [P, OUT1 // P, OUT2])
        wt3_sb = sb("wt3_sb", [P, OUT2 // P])
        bt1_sb = sb("bt1_sb", [P, OUT1 // P])
        bt2_sb = sb("bt2_sb", [P, OUT2 // P])
        h_a = sb("h_a", [P, B])
        h_b = sb("h_b", [H + NCTX, B])
        h1 = x_bc[:, 0:2, :].rearrange("p a (c b) -> p (a c) b", b=B)
        h2 = x_bc[:, 2, :].rearrange("p (c b) -> p c b", b=B)
        upper = x_bc[0:H, 3:5, :].rearrange("p a (c b) -> p (a c) b", b=B)[:, 0:3, :]
        y_sb = x_bc[0:1, 5, 0:B]

        acc = ctx.enter_context(nc.psum_tensor("acc", [P, 2, CH], F32))
        bc = ctx.enter_context(nc.psum_tensor("bc", [P, BC_SLOTS, PAIR], F32))

        s_idx = sem("idx_loaded")
        s_go = sem("gathers_may_start")
        s_gathered = sem("rows_gathered")
        s_const = sem("x_constants_loaded")
        s_w = sem("layer_weights_loaded")
        s_wt = sem("tower_weights_loaded")
        s_w0 = sem("w0_folded")
        s_turned = sem("rows_turned")
        s_hi = sem("hi_split")
        s_rest = sem("rest_left")
        s_mid = sem("mid_split")
        s_lo = sem("lo_split")
        s_xp = [sem(f"parts_in_place_{j}") for j in range(2)]
        s_fill = sem("psum_filled")
        s_copy = sem("replica_copied")
        s_all = sem("x_all_ready")
        s_dram = sem("x_in_dram")
        s_xd = {t: sem(f"replica_{t}_loaded") for t in DMA_TILES}
        s_z1 = sem("layer1_products")
        s_z = sem("products_by_vector")
        s_zp = sem("products_by_gpsimd")
        s_used = sem("vector_products_used")
        s_zp_used = sem("gpsimd_products_used")
        s_layer1 = sem("layer1_accumulated")
        s_xk = {n: sem(f"xk{n}_ready") for n in (1, 2)}
        s_relu = {n: sem(f"relu{n}_ready") for n in (1, 2, 3)}
        s_sum = sem("dims_summed")
        s_fold = sem("pairs_folded")
        s_upper = sem("upper_moved")
        s_h = sem("tower_input_ready")
        s_m1 = sem("tower1_accumulated")
        s_h1 = sem("tower1_ready")
        s_m2 = sem("tower2_accumulated")
        s_h2 = sem("tower2_ready")
        s_m3 = sem("tower3_accumulated")
        s_y = sem("y_ready")
        s_out = sem("out_written")

        block = ctx.enter_context(nc.Block())

        def filled(r, kind, j, t=0):
            return FIRST_FILLS + r * len(REAL_FILLS) + REAL_FILLS.index((kind, j, t)) + 1

        def copied(r, kind, j, t=0):
            return 1 + r * len(COPIES) + COPIES.index((kind, j, t)) + 1

        def product(r, layer, j, t):
            return r * len(DVE_PRODUCTS) + DVE_PRODUCTS.index((layer, j, t)) + 1

        def pool_product(r, layer, j, t):
            return r * len(POOL_PRODUCTS) + POOL_PRODUCTS.index((layer, j, t)) + 1

        def product1(r, j, t):
            return T1 * (2 * r + j) + t + 1

        def parts(r, j):
            return 16 * 2 * PARTS * (r + 1 + j // 2)

        def used(r, layer, j, t):
            return DVE_SLOTS + product(r, layer, j, t)

        def pair(r, j):
            return 2 * r + j + 1

        def fill_slot(kind, j, t=0):
            return FILLS.index((kind, j, t)) % BC_SLOTS

        def product_slot(layer, j, t):
            return DVE_PRODUCTS.index((layer, j, t)) % DVE_SLOTS

        def pool_slot(layer, j, t):
            return POOL_PRODUCTS.index((layer, j, t)) % POOL_SLOTS

        def wait_replica(eng, r, layer, j, t):
            if t in DMA_TILES:
                eng.wait_ge(s_xd[t], 16 * 2 * pair(r, j))
            else:
                eng.wait_ge(s_copy, copied(r, "bc", j, t))

        def rows_of(t):
            return P if t < T1 - 1 else M

        @block.sync
        def _(sp):
            def load_indices(tile):
                sp.dma_start(idx[:], ids.rearrange("(t p) f -> t p f", p=P)[tile]).then_inc(s_idx, 16)

            def place_parts(j, chunks=(0, 1)):
                for c in chunks:
                    for n, part in enumerate((x_hi, x_mid, x_lo)):
                        q = (2 * j + c) * M
                        sp.dma_start(xp[n * M:(n + 1) * M, j, c * CH:(c + 1) * CH],
                                     part[q:q + M, :]).then_inc(s_xp[j], 16)

            load_indices(0)
            sp.dma_start(sel_sb[:], sel).then_inc(s_const, 16)
            sp.dma_start(id_sb[:], ident).then_inc(s_const, 16)
            sp.dma_start(w0_sb[:, 0:T1 - 1, :], w0a[:, 0:T1 - 1, :]).then_inc(s_w, 16)
            sp.dma_start(w0_sb[0:M, T1 - 1, :], w0a[0:M, T1 - 1, :]).then_inc(s_w, 16)
            sp.dma_start(w0b_sb[:], w0b).then_inc(s_w, 16)
            sp.dma_start(w1_sb[:], w1.rearrange("m h k -> (m h) k").rearrange("(t p) k -> p t k", p=P)
                         ).then_inc(s_w, 16)
            sp.dma_start(w2_sb[:], w2.rearrange("m h k -> (m h) k").rearrange("(t p) k -> p t k", p=P)
                         ).then_inc(s_w, 16)
            sp.dma_start(wt1a_sb[:], wt1[0:P, :]).then_inc(s_wt, 16)
            sp.dma_start(wt1b_sb[:], wt1[P:P + H + NCTX, :]).then_inc(s_wt, 16)
            sp.dma_start(wt2_sb[:], wt2.rearrange("(t p) n -> p t n", p=P)).then_inc(s_wt, 16)
            sp.dma_start(wt3_sb[:], wt3).then_inc(s_wt, 16)
            sp.dma_start(bt1_sb[:], bt1).then_inc(s_wt, 16)
            sp.dma_start(bt2_sb[:], bt2).then_inc(s_wt, 16)
            sp.dma_start(h_b[H:H + NCTX, :], ctx_t).then_inc(s_wt, 16)

            def store_x(tile):
                sp.wait_ge(s_all, tile + 1)
                for c in range(2 * PAIR // CH):
                    sp.dma_start(x_dram[tile, :, c * CH:(c + 1) * CH], x_all[c * M:(c + 1) * M, :]
                                 ).then_inc(s_dram, 16)

            def load_replicas(tile, j, t):
                for q in range(2):
                    row = x_dram[tile, 2 * t + q:2 * t + q + 1, j * PAIR:(j + 1) * PAIR]
                    sp.dma_start(x_bc[q * H:(q + 1) * H, t, :], row.to_broadcast([H, PAIR])
                                 ).then_inc(s_xd[t], 16)

            def next_replicas(r, j, tile):
                for t in DMA_TILES:
                    if ("L3", j, t) in DVE_PRODUCTS:
                        sp.wait_ge(s_z, product(r, "L3", j, t))
                    else:
                        sp.wait_ge(s_zp, pool_product(r, "L3", j, t))
                    load_replicas(tile, 1 - j, t)

            sp.wait_ge(s_gathered, 16 * M)
            load_indices(1)
            sp.wait_ge(s_lo, 1)
            place_parts(0)
            store_x(0)
            sp.wait_ge(s_dram, 16 * 4)
            for t in DMA_TILES:
                load_replicas(0, 0, t)
            place_parts(1)

            def round_(r, load, more):
                if more:
                    sp.wait_ge(s_gathered, 16 * M * (r + 2))
                if load:
                    load_indices(r + 2)
                next_replicas(r, 0, r)
                if not more:
                    return
                sp.wait_ge(s_lo, r + 2)
                sp.wait_ge(s_fill, filled(r, "bc", 0, KEPT_TILES[-1]))
                place_parts(0)
                store_x(r + 1)
                sp.wait_ge(s_fill, filled(r, "bc", 1, KEPT_TILES[-1]))
                place_parts(1, (0,))
                sp.wait_ge(s_dram, 16 * 4 * (r + 2))
                place_parts(1, (1,))
                next_replicas(r, 1, r + 1)

            with sp.Fori(0, NT - 2) as r:
                round_(r, True, True)
            round_(NT - 2, False, True)
            round_(NT - 1, False, False)

            sp.wait_ge(s_y, 1)
            sp.dma_start(out.rearrange("b n -> n b"), y_sb).then_inc(s_out, 16)
            sp.wait_ge(s_out, 16)

        @block.gpsimd
        def _(pool):
            def gather(first, last):
                for f in range(first, last):
                    nc.gpsimd.indirect_dma_start(
                        emb[:, f, :], None, tables[f],
                        bass.IndirectOffsetOnAxis(idx[:, f:f + 1], axis=0)).then_inc(s_gathered, 16)

            def multiply(r, layer, j):
                xk, s_ready = (xk1, s_xk[1]) if layer == "L2" else (xk2, s_xk[2])
                pool.wait_ge(s_ready, 4 * pair(r, j))
                for which, _, t in [x for x in POOL_PRODUCTS if x[:2] == (layer, j)]:
                    wait_replica(pool, r, layer, j, t)
                    pool.wait_ge(s_zp_used, pool_product(r, layer, j, t))
                    nc.gpsimd.tensor_tensor(zp[:, pool_slot(layer, j, t), :], x_bc[:, t, :], xk[:],
                                            ALU.mult).then_inc(s_zp, 1)

            def start_gather(tile):
                pool.wait_ge(s_turned, tile)
                pool.wait_ge(s_idx, 16 * (tile + 1))
                nc.gpsimd.sem_inc(s_go, 1)
                gather(0, GATHERS_FIRST)

            def round_(r, rest, more):
                multiply(r, "L2", 0)
                if rest:
                    gather(GATHERS_FIRST, M)
                multiply(r, "L3", 0)
                multiply(r, "L2", 1)
                if more:
                    start_gather(r + 2)
                multiply(r, "L3", 1)

            pool.wait_ge(s_idx, 16)
            gather(0, M)
            start_gather(1)
            with pool.Fori(0, NT - 2) as r:
                round_(r, True, True)
            round_(NT - 2, True, False)
            round_(NT - 1, False, False)

        @block.scalar
        def _(act):
            def copy_bc(r, j, t):
                act.wait_ge(s_z, product(r, "L2", j, t))
                nc.scalar.activation(x_bc[:, t, :], bc[:, fill_slot("bc", j, t), :], ACT.Copy).then_inc(s_copy, 1)

            def copy_rep(r, j):
                act.wait_ge(s_fill, filled(r, "rep", j))
                nc.scalar.activation(x_rep[:], bc[:, fill_slot("rep", j), :], ACT.Copy).then_inc(s_copy, 1)

            def split_hi(n):
                act.wait_ge(s_turned, n)
                nc.scalar.activation(x_hi[:], acc[:, 0, :], ACT.Copy).then_inc(s_hi, 1)

            def keep_x(n):
                act.wait_ge(s_rest, n)
                nc.scalar.activation(x_all[:], acc[:, 0, :], ACT.Copy).then_inc(s_all, 1)

            def split_mid(n):
                act.wait_ge(s_rest, n)
                nc.scalar.activation(x_mid[:], x_rest[:], ACT.Copy).then_inc(s_mid, 1)

            def evacuate(layer, at):
                if layer < 3:
                    xk = (xk1, xk2)[layer - 1]
                    for c in range(2):
                        for half in range(2):
                            nc.scalar.activation(xk[half * H:(half + 1) * H, c * CH:(c + 1) * CH],
                                                 acc[c * H:(c + 1) * H, at, :], ACT.Relu).then_inc(s_xk[layer], 1)
                nc.scalar.activation(relu[:, at, :], acc[:, at, :], ACT.Relu).then_inc(s_relu[layer], 1)

            def pass_(r, j, more, turn):
                for n, t in enumerate(ORDER2):
                    if t in KEPT_TILES:
                        copy_bc(r, j, t)
                    if turn and n == HI_AT:
                        split_hi(r + 2)
                    if turn and n == MID_AT:
                        split_mid(r + 2)
                    if turn and n == KEEP_AT:
                        act.wait_ge(s_dram, 16 * 4 * (r + 1))
                        keep_x(r + 2)
                if more:
                    copy_rep(r, j + 1)
                act.wait_ge(s_used, used(r, "L2", j, ORDER2[-1]))
                evacuate(2, j)
                if more:
                    act.wait_ge(s_layer1, pair(r, j + 1))
                    evacuate(1, 1 - j)
                act.wait_ge(s_used, used(r, "L3", j, ORDER3[-1]))
                evacuate(3, j)

            split_hi(1)
            split_mid(1)
            keep_x(1)
            copy_rep(-1, 2)
            act.wait_ge(s_layer1, 1)
            evacuate(1, 0)
            with act.Fori(0, NT - 1) as r:
                pass_(r, 0, True, False)
                pass_(r, 1, True, True)
            pass_(NT - 1, 0, True, False)
            pass_(NT - 1, 1, False, False)

            act.wait_ge(s_fold, 1)
            nc.scalar.activation(upper, sums[H:P, 0, :, :], ACT.Copy).then_inc(s_upper, 1)
            act.wait_ge(s_wt, 16 * 7)
            for n in range(OUT1 // P):
                act.wait_ge(s_m1, n + 1)
                nc.scalar.activation(h1[:, n, :], bc[:, n // 2, (n % 2) * B:(n % 2 + 1) * B], ACT.Relu,
                                     bias=bt1_sb[:, n:n + 1]).then_inc(s_h1, 1)
            for n in range(OUT2 // P):
                act.wait_ge(s_m2, n + 1)
                nc.scalar.activation(h2[:, n, :], bc[:, 2, n * B:(n + 1) * B], ACT.Relu,
                                     bias=bt2_sb[:, n:n + 1]).then_inc(s_h2, 1)
            act.wait_ge(s_m3, 1)
            nc.scalar.activation(y_sb, acc[0:1, 0, :], ACT.Copy).then_inc(s_y, 1)

        @block.vector
        def _(dve):
            def subtract_hi(n):
                dve.wait_ge(s_hi, n)
                nc.vector.tensor_tensor(x_rest[:], acc[:, 0, :], x_hi[:], ALU.subtract).then_inc(s_rest, 1)

            def split_lo(n):
                dve.wait_ge(s_mid, n)
                nc.vector.tensor_tensor(x_lo[:], x_rest[:], x_mid[:], ALU.subtract).then_inc(s_lo, 1)

            def sum_dims(layer, n, j, tile):
                dve.wait_ge(s_relu[layer], n)
                nc.vector.tensor_reduce(sums[:, j, layer - 1, bass.ts(tile, P)],
                                        relu[:, j, :].rearrange("p (d b) -> p b d", b=P),
                                        AX_X, ALU.add).then_inc(s_sum, 1)

            def multiply1(t, n_fill, slot):
                rows = rows_of(t)
                dve.wait_ge(s_fill, n_fill)
                nc.vector.tensor_tensor(z1[0:rows, t, :], bc[0:rows, slot, :], x_rep[0:rows, :],
                                        ALU.mult).then_inc(s_z1, 1)

            def multiply(r, layer, j, t):
                dve.wait_ge(s_used, product(r, layer, j, t))
                out_z = z[:, product_slot(layer, j, t), :]
                if layer == "L2" and t in KEPT_TILES:
                    dve.wait_ge(s_fill, filled(r, "bc", j, t))
                    x = bc[:, fill_slot("bc", j, t), :]
                else:
                    wait_replica(dve, r, layer, j, t)
                    x = x_bc[:, t, :]
                nc.vector.tensor_tensor(out_z, x, (xk1 if layer == "L2" else xk2)[:], ALU.mult).then_inc(s_z, 1)

            def layer2(r, j, steps, turn=False):
                if 0 in steps:
                    dve.wait_ge(s_xk[1], 4 * pair(r, j))
                for n in steps:
                    if ("L2", j, ORDER2[n]) in DVE_PRODUCTS:
                        multiply(r, "L2", j, ORDER2[n])
                    if turn and n == REST_AT:
                        subtract_hi(r + 2)
                    if turn and n == LO_AT:
                        split_lo(r + 2)

            def layers1_and_3(r, j, more):
                if more:
                    dve.wait_ge(s_copy, copied(r, "rep", j + 1))
                    for t in range(T1):
                        multiply1(t, filled(r, "shift", j + 1, t), fill_slot("shift", j + 1, t))
                dve.wait_ge(s_xk[2], 4 * pair(r, j))
                for n, t in enumerate(ORDER3):
                    if ("L3", j, t) in DVE_PRODUCTS:
                        multiply(r, "L3", j, t)
                    if n == 1:
                        sum_dims(2, pair(r, j), j, r)
                    if more and n == 4:
                        sum_dims(1, pair(r, j + 1), 1 - j, r if j == 0 else r + 1)

            def round_(r, more):
                layer2(r, 0, range(SUM3_AT + 1, T2))
                layers1_and_3(r, 0, True)
                layer2(r, 1, range(SUM3_AT + 1))
                sum_dims(3, pair(r, 0), 0, r)
                layer2(r, 1, range(SUM3_AT + 1, T2), more)
                layers1_and_3(r, 1, more)
                if more:
                    layer2(r + 1, 0, range(SUM3_AT + 1))
                sum_dims(3, pair(r, 1), 1, r)

            dve.wait_ge(s_w, 16 * 5)
            for q, rows, t in ((M, M, 0), (2 * M, 2 * M, 0), (0, M, 1)):
                w, wb = w0_sb[q:q + rows, t:T1 - 1, :], w0b_sb[q:q + rows, t:, :]
                nc.vector.tensor_tensor(w, w, wb, ALU.add).then_inc(s_w0, 1)
            subtract_hi(1)
            split_lo(1)
            dve.wait_ge(s_copy, 1)
            for t in range(T1):
                multiply1(t, filled(-1, "shift", 2, t), fill_slot("shift", 2, t))
            layer2(0, 0, range(SUM3_AT + 1))
            sum_dims(1, 1, 0, 0)
            with dve.Fori(0, NT - 1) as r:
                round_(r, True)
            round_(NT - 1, False)

            dve.wait_ge(s_sum, 6 * NT)
            nc.vector.tensor_tensor(sums[:, 0, :, :], sums[:, 0, :, :], sums[:, 1, :, :],
                                    ALU.add).then_inc(s_fold, 1)
            dve.wait_ge(s_fold, 1)
            dve.wait_ge(s_upper, 1)
            for n, dst in enumerate((h_a[0:H, :], h_a[H:P, :], h_b[0:H, :])):
                nc.vector.tensor_tensor(dst, sums[0:H, 0, n, :], upper[:, n, :], ALU.add).then_inc(s_h, 1)

        @block.tensor
        def _(pe):
            def turn(tile):
                pe.wait_ge(s_gathered, 16 * M * (tile + 1))
                for dd, c in np.ndindex(DC, D // DC):
                    d = c * DC + dd
                    mm = nc.tensor.matmul(acc[c * M:(c + 1) * M, 0, dd * P:(dd + 1) * P], emb[:, :, d],
                                          id_sb[:], start=True, stop=True)
                mm.then_inc(s_turned, 1)

            def replicate(slot, kind, j, t):
                n = {"rep": 0, "shift": 1 + t, "bc": 1 + T1 + t}[kind]
                for c in range(2):
                    mm = nc.tensor.matmul(bc[:, slot, c * CH:(c + 1) * CH], sel_sb[:, n * P:(n + 1) * P],
                                          xp[:, j % 2, c * CH:(c + 1) * CH], start=True, stop=True)
                mm.then_inc(s_fill, 1)

            def fill(r, n):
                if FILLS[n % len(FILLS)][0] == "none":
                    return
                kind, j, t = FILLS[n - BC_SLOTS]
                if kind in ("bc", "rep"):
                    pe.wait_ge(s_copy, copied(r, kind, j, t))
                if kind == "shift":
                    pe.wait_ge(s_z1, product1(r, j, t))
                kind, j, t = FILLS[n % len(FILLS)]
                if kind == "rep":
                    pe.wait_ge(s_xp[j % 2], parts(r, j))
                replicate(n % BC_SLOTS, kind, j, t)

            def fill_after(r, kind, j, t, more):
                n = FILLS.index((kind, j, t)) + BC_SLOTS
                if more or n < FILLS.index(("rep", 2, 0)):
                    fill(r, n)

            def accumulate(zt, w, at, first, last):
                for c in range(2):
                    mm = nc.tensor.matmul(acc[c * H:(c + 1) * H, at, :], w, zt[:, c * CH:(c + 1) * CH],
                                          start=first, stop=last)
                return mm

            def layer23(r, layer, j, t, n):
                w = (w1_sb if layer == "L2" else w2_sb)[:, t, :]
                if (layer, j, t) in DVE_PRODUCTS:
                    pe.wait_ge(s_z, product(r, layer, j, t))
                    zt, s_done = z[:, product_slot(layer, j, t), :], s_used
                else:
                    pe.wait_ge(s_zp, pool_product(r, layer, j, t))
                    zt, s_done = zp[:, pool_slot(layer, j, t), :], s_zp_used
                accumulate(zt, w, j, n == 0, n == T2 - 1).then_inc(s_done, 1)

            def layer1(r, j, more):
                fill_after(r, "rep", j, 0, more)
                for t in range(T1):
                    pe.wait_ge(s_z1, product1(r, j, t))
                    rows = rows_of(t)
                    mm = accumulate(z1[0:rows, t, :], w0_sb[0:rows, t, :], j % 2, t == 0, t == T1 - 1)
                    if t == T1 - 1:
                        mm.then_inc(s_layer1, 1)
                    fill_after(r, "shift", j, t, more)
                if j == 2:
                    for n, (kind, _, _) in enumerate(FILLS):
                        if kind == "none":
                            fill(r, n + BC_SLOTS)

            def pass_(r, j, more, with_turn):
                pe.wait_ge(s_relu[1], pair(r, j))
                for n, t in enumerate(ORDER2):
                    layer23(r, "L2", j, t, n)
                    if t in KEPT_TILES and FILLS[FILLS.index(("bc", j, t)) + BC_SLOTS][0] == "bc":
                        fill_after(r, "bc", j, t, more)
                    if n in AHEAD and (more or j == 0):
                        fill(r, FILLS.index(("rep", j + 1, 0)) + AHEAD.index(n))
                    if with_turn and n == TURN_AT:
                        pe.wait_ge(s_relu[3], pair(r, 0))
                        turn(r + 1)
                if j == 0:
                    layer1(r, 1, more)
                elif more:
                    pe.wait_ge(s_all, r + 2)
                    layer1(r, 2, more)
                pe.wait_ge(s_relu[2], pair(r, j))
                for n, t in enumerate(ORDER3):
                    layer23(r, "L3", j, t, n)

            pe.wait_ge(s_const, 16 * 2)
            turn(0)
            pe.wait_ge(s_xp[0], parts(-1, 2))
            for n, (kind, j, t) in enumerate(FILLS):
                if (kind, j) == ("rep", 2) or (kind, j) == ("shift", 2) and t < BC_SLOTS - 1:
                    mm = replicate(n % BC_SLOTS, kind, j, t)
            pe.wait_ge(s_w, 16 * 5)
            pe.wait_ge(s_w0, 3)
            nc.tensor.sem_inc(s_used, DVE_SLOTS)
            nc.tensor.sem_inc(s_zp_used, POOL_SLOTS)
            layer1(-1, 2, True)
            with pe.Fori(0, NT - 1) as r:
                pass_(r, 0, True, False)
                pass_(r, 1, True, True)
            pass_(NT - 1, 0, False, False)
            pass_(NT - 1, 1, False, False)

            pe.wait_ge(s_wt, 16 * 7)
            pe.wait_ge(s_h, 3)
            for n in range(OUT1 // P):
                dst = bc[:, n // 2, (n % 2) * B:(n % 2 + 1) * B]
                nc.tensor.matmul(dst, wt1a_sb[:, n * P:(n + 1) * P], h_a[:], start=True, stop=False)
                nc.tensor.matmul(dst, wt1b_sb[:, n * P:(n + 1) * P], h_b[:], start=False,
                                 stop=True).then_inc(s_m1, 1)
            for n in range(OUT2 // P):
                for c in range(OUT1 // P):
                    pe.wait_ge(s_h1, c + 1)
                    mm = nc.tensor.matmul(bc[:, 2, n * B:(n + 1) * B], wt2_sb[:, c, n * P:(n + 1) * P],
                                          h1[:, c, :], start=(c == 0), stop=(c == OUT1 // P - 1))
                mm.then_inc(s_m2, 1)
            for c in range(OUT2 // P):
                pe.wait_ge(s_h2, c + 1)
                mm = nc.tensor.matmul(acc[0:1, 0, :], wt3_sb[:, c:c + 1], h2[:, c, :],
                                      start=(c == 0), stop=(c == OUT2 // P - 1))
            mm.then_inc(s_m3, 1)


def selections():
    q = np.arange(P)
    rows = [q % M]
    rows += [(q % M + 4 * t + q // M) % M for t in range(T1)]
    rows += [2 * t + q // H for t in range(T2)]
    return np.concatenate([(np.arange(PARTS * M)[:, None] % M == r[None, :]) for r in rows], axis=1)


def kernel(**inputs):
    import ml_dtypes
    import concourse.bacc as bacc
    from concourse.bass_utils import run_bass_kernel_spmd

    nc = bacc.Bacc("TRN2", target_bir_lowering=False, num_devices=1)
    arrays = {}

    def give(name, a):
        a = np.ascontiguousarray(a)
        arrays[name] = a
        return nc.dram_tensor(name, a.shape, mybir.dt.from_np(a.dtype), kind="ExternalInput").ap()

    w0 = np.asarray(inputs["L0_rec_W0"])
    m = np.arange(M)
    shift = np.arange(M // 2 + 1)[:, None]
    direct = w0[m[None, :], (m[None, :] + shift) % M]
    mirror = w0[(m[None, :] + shift) % M, m[None, :]]
    tiled = [a[:16].reshape(4, P, H).transpose(1, 0, 2) for a in (direct, mirror)]
    last = direct[M // 2, np.arange(P) % M][:, None, :]
    args = [
        give("ids_dram", inputs["ids"]),
        [give(f"tbl_{f}_dram", inputs[f"tbl_{f}"]) for f in range(M)],
        give("sel_dram", selections().astype(ml_dtypes.bfloat16)),
        give("ident_dram", np.eye(P, dtype=np.float32)),
        give("w0a_dram", np.concatenate([tiled[0], last], axis=1)),
        give("w0b_dram", tiled[1]),
        give("w1_dram", inputs["L0_rec_W1"]),
        give("w2_dram", inputs["L0_rec_W2"]),
        give("ctx_dram", np.asarray(inputs["dense_ctx"]).T),
        give("wt1_dram", inputs["W_top1"]),
        give("bt1_dram", np.asarray(inputs["b_top1"]).reshape(OUT1 // P, P).T),
        give("wt2_dram", inputs["W_top2"]),
        give("bt2_dram", np.asarray(inputs["b_top2"]).reshape(OUT2 // P, P).T),
        give("wt3_dram", np.asarray(inputs["W_top3"]).reshape(OUT2 // P, P).T),
    ]
    out = nc.dram_tensor("out_dram", (B, 1), F32, kind="ExternalOutput").ap()
    x_dram = nc.dram_tensor("x_dram", (NT, M, 2 * PAIR), F32).ap()
    interaction_tower(nc, *args, x_dram, out)
    return run_bass_kernel_spmd(nc, [arrays], core_ids=[0]).results[0]["out_dram"]
```

```python
from contextlib import ExitStack

import numpy as np

import concourse.bass as bass
from concourse import mybir

F32 = mybir.dt.float32
BF16 = mybir.dt.bfloat16
I32 = mybir.dt.int32
ALU = mybir.AluOpType
ACT = mybir.ActivationFunctionType
AX_X = mybir.AxisListType.X

B, M, D, H = 512, 32, 16, 64
P = 128
NT = B // P
CH = 512
DC = CH // P
PAIR = 2 * CH
NPAIR = D * P // PAIR
OUT1, OUT2, NCTX = 512, 256, 16

T1 = 5
T2 = M * H // P
PARTS = 3

DMA_TILES = (3, 4, 5, 6, 7, 8, 9, 10, 11, 12, 13, 14, 15)
KEPT_TILES = tuple(t for t in range(T2) if t not in DMA_TILES)
ORDER2 = (3, 4, 5, 0, 6, 7, 8, 1, 9, 10, 11, 2, 12, 13, 14, 15)
ORDER3 = DMA_TILES + KEPT_TILES
POOL_TILES = {("L2", 0): (5, 8, 11), ("L3", 0): (5, 8, 11, 14, 0),
              ("L2", 1): (5, 8, 11), ("L3", 1): (5, 8, 11, 14, 0)}
DVE_SLOTS = 6
POOL_SLOTS = 4
BC_SLOTS = 3
GATHERS_FIRST = 16
TURN_AT, HI_AT, REST_AT, MID_AT, LO_AT, KEEP_AT = 3, 4, 7, 8, 9, 9
AHEAD = (13, 14, 15)
TOWER2_AT, TOWER3_AT = (4, 7), 11
FOLD_AT, ADD_AT = 4, 8
SUM3_AT = 4


def fill_order():
    order = []
    for j in range(2):
        order += [("bc", j, t) for t in ORDER2 if t in KEPT_TILES]
        order += [("rep", j + 1, 0)] + [("shift", j + 1, t) for t in range(T1)]
    return order + [("none", 2, 0)] * (-len(order) % BC_SLOTS)


FILLS = fill_order()
REAL_FILLS = [x for x in FILLS if x[0] != "none"]
FIRST_FILLS = 1 + T1
COPIES = [x for x in FILLS if x[0] in ("bc", "rep")]
PRODUCTS = [(layer, j, t) for j in range(2) for layer, order in (("L2", ORDER2), ("L3", ORDER3)) for t in order]
DVE_PRODUCTS = [x for x in PRODUCTS if x[2] not in POOL_TILES[x[:2]]]
POOL_PRODUCTS = [x for x in PRODUCTS if x[2] in POOL_TILES[x[:2]]]
assert len(AHEAD) == BC_SLOTS
assert len(DVE_PRODUCTS) % DVE_SLOTS == 0 and len(POOL_PRODUCTS) % POOL_SLOTS == 0
assert all(("L2", j, ORDER2[-1]) in DVE_PRODUCTS and ("L3", j, ORDER3[-1]) in DVE_PRODUCTS for j in range(2))
assert all(x in DVE_PRODUCTS for x in PRODUCTS if x[0] == "L2" and x[2] in KEPT_TILES)


def interaction_tower(nc, ids, tables, sel, ident, w0a, w0b, w1, w2, ctx_t,
                      wt1, bt1, wt2, bt2, wt3, x_dram, out):
    with ExitStack() as ctx:
        def sb(name, shape, dt=F32):
            return ctx.enter_context(nc.sbuf_tensor(name, shape, dt))

        def sem(name):
            return ctx.enter_context(nc.semaphore(name))

        idx = sb("idx", [P, M], I32)
        emb = sb("emb", [P, M, D])
        sel_sb = sb("sel_sb", [PARTS * M, sel.shape[1]], BF16)
        id_sb = sb("id_sb", [P, P])
        x_hi = sb("x_hi", [P, CH], BF16)
        x_mid = sb("x_mid", [P, CH], BF16)
        x_lo = sb("x_lo", [P, CH], BF16)
        x_rest = sb("x_rest", [P, CH])
        xp = sb("xp", [PARTS * M, 2, PAIR], BF16)
        x_rep = sb("x_rep", [P, PAIR])
        x_all = sb("x_all", [P, CH])
        x_bc = sb("x_bc", [P, T2, PAIR])
        xk1 = sb("xk1", [P, PAIR])
        xk2 = sb("xk2", [P, PAIR])
        z1 = sb("z1", [P, T1, PAIR])
        z = sb("z", [P, DVE_SLOTS, PAIR])
        zp = sb("zp", [P, POOL_SLOTS, PAIR])
        relu = sb("relu", [P, 2, CH])
        sums = sb("sums", [P, 2, 3, B])
        w0_sb = sb("w0_sb", [P, T1, H])
        w0b_sb = sb("w0b_sb", [P, T1 - 1, H])
        w1_sb = sb("w1_sb", [P, T2, H])
        w2_sb = sb("w2_sb", [P, T2, H])
        wt1a_sb = sb("wt1a_sb", [P, OUT1])
        wt1b_sb = sb("wt1b_sb", [H + NCTX, OUT1])
        wt1c_sb = sb("wt1c_sb", [P, OUT1])
        wt2_sb = sb("wt2_sb", [P, OUT1 // P, OUT2])
        wt3_sb = sb("wt3_sb", [P, OUT2 // P])
        bt1_sb = sb("bt1_sb", [P, OUT1 // P])
        bt2_sb = sb("bt2_sb", [P, OUT2 // P])
        h_a = sb("h_a", [P, B])
        h_b = sb("h_b", [H + NCTX, B])
        h1 = z1[:, 0:2, :].rearrange("p a (c b) -> p (a c) b", b=B)
        h2 = z1[:, 2, :].rearrange("p (c b) -> p c b", b=B)
        upper = z1[0:H, 3:5, :].rearrange("p a (c b) -> p (a c) b", b=B)[:, 0:3, :]
        y_sb = z1[0:1, 4, B:2 * B]

        acc = ctx.enter_context(nc.psum_tensor("acc", [P, 2, CH], F32))
        bc = ctx.enter_context(nc.psum_tensor("bc", [P, BC_SLOTS, PAIR], F32))

        s_idx = sem("idx_loaded")
        s_go = sem("gathers_may_start")
        s_gathered = sem("rows_gathered")
        s_const = sem("x_constants_loaded")
        s_w = sem("layer_weights_loaded")
        s_wt = sem("tower_weights_loaded")
        s_w0 = sem("w0_folded")
        s_turned = sem("rows_turned")
        s_hi = sem("hi_split")
        s_rest = sem("rest_left")
        s_mid = sem("mid_split")
        s_lo = sem("lo_split")
        s_xp = [sem(f"parts_in_place_{j}") for j in range(2)]
        s_fill = sem("psum_filled")
        s_copy = sem("replica_copied")
        s_all = sem("x_all_ready")
        s_dram = sem("x_in_dram")
        s_xd = {t: sem(f"replica_{t}_loaded") for t in DMA_TILES}
        s_z1 = sem("layer1_products")
        s_z = sem("products_by_vector")
        s_zp = sem("products_by_gpsimd")
        s_used = sem("vector_products_used")
        s_zp_used = sem("gpsimd_products_used")
        s_layer1 = sem("layer1_accumulated")
        s_xk = {n: sem(f"xk{n}_ready") for n in (1, 2)}
        s_relu = {n: sem(f"relu{n}_ready") for n in (1, 2, 3)}
        s_sum = sem("dims_summed")
        s_fold = sem("pairs_folded")
        s_upper = sem("upper_moved")
        s_h = sem("tower_input_ready")
        s_m1 = sem("tower1_accumulated")
        s_h1 = sem("tower1_ready")
        s_m2 = sem("tower2_accumulated")
        s_h2 = sem("tower2_ready")
        s_m3 = sem("tower3_accumulated")
        s_y = sem("y_ready")
        s_out = sem("out_written")

        block = ctx.enter_context(nc.Block())

        def filled(r, kind, j, t=0):
            return FIRST_FILLS + r * len(REAL_FILLS) + REAL_FILLS.index((kind, j, t)) + 1

        def copied(r, kind, j, t=0):
            return 1 + r * len(COPIES) + COPIES.index((kind, j, t)) + 1

        def product(r, layer, j, t):
            return r * len(DVE_PRODUCTS) + DVE_PRODUCTS.index((layer, j, t)) + 1

        def pool_product(r, layer, j, t):
            return r * len(POOL_PRODUCTS) + POOL_PRODUCTS.index((layer, j, t)) + 1

        def product1(r, j, t):
            return T1 * (2 * r + j) + t + 1

        def parts(r, j):
            return 16 * 2 * PARTS * (r + 1 + j // 2)

        def used(r, layer, j, t):
            return DVE_SLOTS + product(r, layer, j, t)

        def pair(r, j):
            return 2 * r + j + 1

        tower_parts = (slice(0, B - P), slice(B - P, B))

        def tower1_psum(n):
            return bc[:, n // 2, (n % 2) * B:(n % 2 + 1) * B]

        def fill_slot(kind, j, t=0):
            return FILLS.index((kind, j, t)) % BC_SLOTS

        def product_slot(layer, j, t):
            return DVE_PRODUCTS.index((layer, j, t)) % DVE_SLOTS

        def pool_slot(layer, j, t):
            return POOL_PRODUCTS.index((layer, j, t)) % POOL_SLOTS

        def wait_replica(eng, r, layer, j, t):
            if t in DMA_TILES:
                eng.wait_ge(s_xd[t], 16 * 2 * pair(r, j))
            else:
                eng.wait_ge(s_copy, copied(r, "bc", j, t))

        def rows_of(t):
            return P if t < T1 - 1 else M

        @block.sync
        def _(sp):
            def load_indices(tile):
                sp.dma_start(idx[:], ids.rearrange("(t p) f -> t p f", p=P)[tile]).then_inc(s_idx, 16)

            def place_parts(j, chunks=(0, 1)):
                for c in chunks:
                    for n, part in enumerate((x_hi, x_mid, x_lo)):
                        q = (2 * j + c) * M
                        sp.dma_start(xp[n * M:(n + 1) * M, j, c * CH:(c + 1) * CH],
                                     part[q:q + M, :]).then_inc(s_xp[j], 16)

            load_indices(0)
            sp.dma_start(sel_sb[:], sel).then_inc(s_const, 16)
            sp.dma_start(id_sb[:], ident).then_inc(s_const, 16)
            sp.dma_start(w0_sb[:, 0:T1 - 1, :], w0a[:, 0:T1 - 1, :]).then_inc(s_w, 16)
            sp.dma_start(w0_sb[0:M, T1 - 1, :], w0a[0:M, T1 - 1, :]).then_inc(s_w, 16)
            sp.dma_start(w0b_sb[:], w0b).then_inc(s_w, 16)
            sp.dma_start(w1_sb[:], w1.rearrange("m h k -> (m h) k").rearrange("(t p) k -> p t k", p=P)
                         ).then_inc(s_w, 16)
            sp.dma_start(w2_sb[:], w2.rearrange("m h k -> (m h) k").rearrange("(t p) k -> p t k", p=P)
                         ).then_inc(s_w, 16)
            sp.dma_start(wt1a_sb[:], wt1[0:P, :]).then_inc(s_wt, 16)
            sp.dma_start(wt1b_sb[:], wt1[P:P + H + NCTX, :]).then_inc(s_wt, 16)
            for q in range(2):
                sp.dma_start(wt1c_sb[q * H:(q + 1) * H, :], wt1[P:P + H, :]).then_inc(s_wt, 16)
            sp.dma_start(wt2_sb[:], wt2.rearrange("(t p) n -> p t n", p=P)).then_inc(s_wt, 16)
            sp.dma_start(wt3_sb[:], wt3).then_inc(s_wt, 16)
            sp.dma_start(bt1_sb[:], bt1).then_inc(s_wt, 16)
            sp.dma_start(bt2_sb[:], bt2).then_inc(s_wt, 16)
            sp.dma_start(h_b[H:H + NCTX, :], ctx_t).then_inc(s_wt, 16)

            def store_x(tile):
                sp.wait_ge(s_all, tile + 1)
                for c in range(2 * PAIR // CH):
                    sp.dma_start(x_dram[tile, :, c * CH:(c + 1) * CH], x_all[c * M:(c + 1) * M, :]
                                 ).then_inc(s_dram, 16)

            def load_replicas(tile, j, t):
                for q in range(2):
                    row = x_dram[tile, 2 * t + q:2 * t + q + 1, j * PAIR:(j + 1) * PAIR]
                    sp.dma_start(x_bc[q * H:(q + 1) * H, t, :], row.to_broadcast([H, PAIR])
                                 ).then_inc(s_xd[t], 16)

            def next_replicas(r, j, tile):
                for t in DMA_TILES:
                    if ("L3", j, t) in DVE_PRODUCTS:
                        sp.wait_ge(s_z, product(r, "L3", j, t))
                    else:
                        sp.wait_ge(s_zp, pool_product(r, "L3", j, t))
                    load_replicas(tile, 1 - j, t)

            sp.wait_ge(s_gathered, 16 * M)
            load_indices(1)
            sp.wait_ge(s_lo, 1)
            place_parts(0)
            store_x(0)
            sp.wait_ge(s_dram, 16 * 4)
            for t in DMA_TILES:
                load_replicas(0, 0, t)
            place_parts(1)

            def round_(r, load, more):
                if more:
                    sp.wait_ge(s_gathered, 16 * M * (r + 2))
                if load:
                    load_indices(r + 2)
                next_replicas(r, 0, r)
                if not more:
                    return
                sp.wait_ge(s_lo, r + 2)
                sp.wait_ge(s_fill, filled(r, "bc", 0, KEPT_TILES[-1]))
                place_parts(0)
                store_x(r + 1)
                sp.wait_ge(s_fill, filled(r, "bc", 1, KEPT_TILES[-1]))
                place_parts(1, (0,))
                sp.wait_ge(s_dram, 16 * 4 * (r + 2))
                place_parts(1, (1,))
                next_replicas(r, 1, r + 1)

            with sp.Fori(0, NT - 2) as r:
                round_(r, True, True)
            round_(NT - 2, False, True)
            round_(NT - 1, False, False)

            sp.wait_ge(s_y, 2)
            sp.dma_start(out.rearrange("b n -> n b"), y_sb).then_inc(s_out, 16)
            sp.wait_ge(s_out, 16)

        @block.gpsimd
        def _(pool):
            def gather(first, last):
                for f in range(first, last):
                    nc.gpsimd.indirect_dma_start(
                        emb[:, f, :], None, tables[f],
                        bass.IndirectOffsetOnAxis(idx[:, f:f + 1], axis=0)).then_inc(s_gathered, 16)

            def multiply(r, layer, j):
                xk, s_ready = (xk1, s_xk[1]) if layer == "L2" else (xk2, s_xk[2])
                pool.wait_ge(s_ready, 4 * pair(r, j))
                for which, _, t in [x for x in POOL_PRODUCTS if x[:2] == (layer, j)]:
                    wait_replica(pool, r, layer, j, t)
                    pool.wait_ge(s_zp_used, pool_product(r, layer, j, t))
                    nc.gpsimd.tensor_tensor(zp[:, pool_slot(layer, j, t), :], x_bc[:, t, :], xk[:],
                                            ALU.mult).then_inc(s_zp, 1)

            def start_gather(tile):
                pool.wait_ge(s_turned, tile)
                pool.wait_ge(s_idx, 16 * (tile + 1))
                nc.gpsimd.sem_inc(s_go, 1)
                gather(0, GATHERS_FIRST)

            def round_(r, rest, more):
                multiply(r, "L2", 0)
                if rest:
                    gather(GATHERS_FIRST, M)
                multiply(r, "L3", 0)
                multiply(r, "L2", 1)
                if more:
                    start_gather(r + 2)
                multiply(r, "L3", 1)

            pool.wait_ge(s_idx, 16)
            gather(0, M)
            start_gather(1)
            with pool.Fori(0, NT - 2) as r:
                round_(r, True, True)
            round_(NT - 2, True, False)
            round_(NT - 1, False, False)

        @block.scalar
        def _(act):
            def copy_bc(r, j, t):
                act.wait_ge(s_z, product(r, "L2", j, t))
                nc.scalar.activation(x_bc[:, t, :], bc[:, fill_slot("bc", j, t), :], ACT.Copy).then_inc(s_copy, 1)

            def copy_rep(r, j):
                act.wait_ge(s_fill, filled(r, "rep", j))
                nc.scalar.activation(x_rep[:], bc[:, fill_slot("rep", j), :], ACT.Copy).then_inc(s_copy, 1)

            def split_hi(n):
                act.wait_ge(s_turned, n)
                nc.scalar.activation(x_hi[:], acc[:, 0, :], ACT.Copy).then_inc(s_hi, 1)

            def keep_x(n):
                act.wait_ge(s_rest, n)
                nc.scalar.activation(x_all[:], acc[:, 0, :], ACT.Copy).then_inc(s_all, 1)

            def split_mid(n):
                act.wait_ge(s_rest, n)
                nc.scalar.activation(x_mid[:], x_rest[:], ACT.Copy).then_inc(s_mid, 1)

            def evacuate(layer, at):
                if layer < 3:
                    xk = (xk1, xk2)[layer - 1]
                    for c in range(2):
                        for half in range(2):
                            nc.scalar.activation(xk[half * H:(half + 1) * H, c * CH:(c + 1) * CH],
                                                 acc[c * H:(c + 1) * H, at, :], ACT.Relu).then_inc(s_xk[layer], 1)
                nc.scalar.activation(relu[:, at, :], acc[:, at, :], ACT.Relu).then_inc(s_relu[layer], 1)

            def move_upper(part):
                act.wait_ge(s_fold, part + 1)
                cols = tower_parts[part]
                nc.scalar.activation(upper[:, :, cols], sums[H:P, 0, :, cols], ACT.Copy).then_inc(s_upper, 1)

            def tower1(part):
                cols = tower_parts[part]
                for n in range(OUT1 // P):
                    act.wait_ge(s_m1, (OUT1 // P) * part + n + 1)
                    nc.scalar.activation(h1[:, n, cols], tower1_psum(n)[:, cols], ACT.Relu,
                                         bias=bt1_sb[:, n:n + 1]).then_inc(s_h1, 1)

            def tower2_and_3(part):
                cols = tower_parts[part]
                for n in range(OUT2 // P):
                    act.wait_ge(s_m2, (OUT2 // P) * part + n + 1)
                    nc.scalar.activation(h2[:, n, cols], bc[:, 2, n * B:(n + 1) * B][:, cols], ACT.Relu,
                                         bias=bt2_sb[:, n:n + 1]).then_inc(s_h2, 1)
                act.wait_ge(s_m3, part + 1)
                nc.scalar.activation(y_sb[:, cols], acc[0:1, 0, cols], ACT.Copy).then_inc(s_y, 1)

            def pass_(r, j, more, turn, last=False):
                for n, t in enumerate(ORDER2):
                    if t in KEPT_TILES:
                        copy_bc(r, j, t)
                    if last and n == 7:
                        move_upper(0)
                    if turn and n == HI_AT:
                        split_hi(r + 2)
                    if turn and n == MID_AT:
                        split_mid(r + 2)
                    if turn and n == KEEP_AT:
                        act.wait_ge(s_dram, 16 * 4 * (r + 1))
                        keep_x(r + 2)
                if more:
                    copy_rep(r, j + 1)
                act.wait_ge(s_used, used(r, "L2", j, ORDER2[-1]))
                evacuate(2, j)
                if more:
                    act.wait_ge(s_layer1, pair(r, j + 1))
                    evacuate(1, 1 - j)
                if last:
                    act.wait_ge(s_wt, 16 * 9)
                    tower1(0)
                    move_upper(1)
                    tower2_and_3(0)
                act.wait_ge(s_used, used(r, "L3", j, ORDER3[-1]))
                evacuate(3, j)

            split_hi(1)
            split_mid(1)
            keep_x(1)
            copy_rep(-1, 2)
            act.wait_ge(s_layer1, 1)
            evacuate(1, 0)
            with act.Fori(0, NT - 1) as r:
                pass_(r, 0, True, False)
                pass_(r, 1, True, True)
            pass_(NT - 1, 0, True, False)
            pass_(NT - 1, 1, False, False, True)
            tower1(1)
            tower2_and_3(1)

        @block.vector
        def _(dve):
            def subtract_hi(n):
                dve.wait_ge(s_hi, n)
                nc.vector.tensor_tensor(x_rest[:], acc[:, 0, :], x_hi[:], ALU.subtract).then_inc(s_rest, 1)

            def split_lo(n):
                dve.wait_ge(s_mid, n)
                nc.vector.tensor_tensor(x_lo[:], x_rest[:], x_mid[:], ALU.subtract).then_inc(s_lo, 1)

            def sum_dims(layer, n, j, tile):
                dve.wait_ge(s_relu[layer], n)
                nc.vector.tensor_reduce(sums[:, j, layer - 1, bass.ts(tile, P)],
                                        relu[:, j, :].rearrange("p (d b) -> p b d", b=P),
                                        AX_X, ALU.add).then_inc(s_sum, 1)

            def multiply1(t, n_fill, slot):
                rows = rows_of(t)
                dve.wait_ge(s_fill, n_fill)
                nc.vector.tensor_tensor(z1[0:rows, t, :], bc[0:rows, slot, :], x_rep[0:rows, :],
                                        ALU.mult).then_inc(s_z1, 1)

            def multiply(r, layer, j, t):
                dve.wait_ge(s_used, product(r, layer, j, t))
                out_z = z[:, product_slot(layer, j, t), :]
                if layer == "L2" and t in KEPT_TILES:
                    dve.wait_ge(s_fill, filled(r, "bc", j, t))
                    x = bc[:, fill_slot("bc", j, t), :]
                else:
                    wait_replica(dve, r, layer, j, t)
                    x = x_bc[:, t, :]
                nc.vector.tensor_tensor(out_z, x, (xk1 if layer == "L2" else xk2)[:], ALU.mult).then_inc(s_z, 1)

            def fold_pairs(part):
                dve.wait_ge(s_sum, 6 * (NT - 1) + (1 if part == 0 else 5))
                cols, layers = tower_parts[part], slice(0, 3 - part)
                nc.vector.tensor_tensor(sums[:, 0, layers, cols], sums[:, 0, layers, cols],
                                        sums[:, 1, layers, cols], ALU.add).then_inc(s_fold, 1)

            def add_chunks(part):
                dve.wait_ge(s_upper, part + 1)
                dve.wait_ge(s_fold, part + 1)
                cols = tower_parts[part]
                for n, dst in enumerate((h_a[0:H, cols], h_a[H:P, cols], h_b[0:H, cols])):
                    nc.vector.tensor_tensor(dst, sums[0:H, 0, n, cols], upper[:, n, cols], ALU.add).then_inc(s_h, 1)

            def layer2(r, j, steps, turn=False):
                if 0 in steps:
                    dve.wait_ge(s_xk[1], 4 * pair(r, j))
                for n in steps:
                    if ("L2", j, ORDER2[n]) in DVE_PRODUCTS:
                        multiply(r, "L2", j, ORDER2[n])
                    if turn and n == REST_AT:
                        subtract_hi(r + 2)
                    if turn and n == LO_AT:
                        split_lo(r + 2)

            def layers1_and_3(r, j, more):
                if more:
                    dve.wait_ge(s_copy, copied(r, "rep", j + 1))
                    for t in range(T1):
                        multiply1(t, filled(r, "shift", j + 1, t), fill_slot("shift", j + 1, t))
                dve.wait_ge(s_xk[2], 4 * pair(r, j))
                for n, t in enumerate(ORDER3):
                    if ("L3", j, t) in DVE_PRODUCTS:
                        multiply(r, "L3", j, t)
                    if n == 1:
                        sum_dims(2, pair(r, j), j, r)
                    if more and n == 4:
                        sum_dims(1, pair(r, j + 1), 1 - j, r if j == 0 else r + 1)
                    if not more and n == FOLD_AT:
                        fold_pairs(1)
                    if not more and n == ADD_AT:
                        add_chunks(1)

            def round_(r, more):
                layer2(r, 0, range(SUM3_AT + 1, T2))
                layers1_and_3(r, 0, True)
                if not more:
                    fold_pairs(0)
                layer2(r, 1, range(SUM3_AT + 1))
                sum_dims(3, pair(r, 0), 0, r)
                layer2(r, 1, range(SUM3_AT + 1, T2), more)
                if not more:
                    add_chunks(0)
                layers1_and_3(r, 1, more)
                if more:
                    layer2(r + 1, 0, range(SUM3_AT + 1))
                sum_dims(3, pair(r, 1), 1, r)

            dve.wait_ge(s_w, 16 * 5)
            for q, rows, t in ((M, M, 0), (2 * M, 2 * M, 0), (0, M, 1)):
                w, wb = w0_sb[q:q + rows, t:T1 - 1, :], w0b_sb[q:q + rows, t:, :]
                nc.vector.tensor_tensor(w, w, wb, ALU.add).then_inc(s_w0, 1)
            subtract_hi(1)
            split_lo(1)
            dve.wait_ge(s_copy, 1)
            for t in range(T1):
                multiply1(t, filled(-1, "shift", 2, t), fill_slot("shift", 2, t))
            layer2(0, 0, range(SUM3_AT + 1))
            sum_dims(1, 1, 0, 0)
            with dve.Fori(0, NT - 1) as r:
                round_(r, True)
            round_(NT - 1, False)

        @block.tensor
        def _(pe):
            def turn(tile):
                pe.wait_ge(s_gathered, 16 * M * (tile + 1))
                for dd, c in np.ndindex(DC, D // DC):
                    d = c * DC + dd
                    mm = nc.tensor.matmul(acc[c * M:(c + 1) * M, 0, dd * P:(dd + 1) * P], emb[:, :, d],
                                          id_sb[:], start=True, stop=True)
                mm.then_inc(s_turned, 1)

            def replicate(slot, kind, j, t):
                n = {"rep": 0, "shift": 1 + t, "bc": 1 + T1 + t}[kind]
                for c in range(2):
                    mm = nc.tensor.matmul(bc[:, slot, c * CH:(c + 1) * CH], sel_sb[:, n * P:(n + 1) * P],
                                          xp[:, j % 2, c * CH:(c + 1) * CH], start=True, stop=True)
                mm.then_inc(s_fill, 1)

            def fill(r, n):
                if FILLS[n % len(FILLS)][0] == "none":
                    return
                kind, j, t = FILLS[n - BC_SLOTS]
                if kind in ("bc", "rep"):
                    pe.wait_ge(s_copy, copied(r, kind, j, t))
                if kind == "shift":
                    pe.wait_ge(s_z1, product1(r, j, t))
                kind, j, t = FILLS[n % len(FILLS)]
                if kind == "rep":
                    pe.wait_ge(s_xp[j % 2], parts(r, j))
                replicate(n % BC_SLOTS, kind, j, t)

            def fill_after(r, kind, j, t, more):
                n = FILLS.index((kind, j, t)) + BC_SLOTS
                if more or n < FILLS.index(("rep", 2, 0)):
                    fill(r, n)

            def accumulate(zt, w, at, first, last):
                for c in range(2):
                    mm = nc.tensor.matmul(acc[c * H:(c + 1) * H, at, :], w, zt[:, c * CH:(c + 1) * CH],
                                          start=first, stop=last)
                return mm

            def layer23(r, layer, j, t, n):
                w = (w1_sb if layer == "L2" else w2_sb)[:, t, :]
                if (layer, j, t) in DVE_PRODUCTS:
                    pe.wait_ge(s_z, product(r, layer, j, t))
                    zt, s_done = z[:, product_slot(layer, j, t), :], s_used
                else:
                    pe.wait_ge(s_zp, pool_product(r, layer, j, t))
                    zt, s_done = zp[:, pool_slot(layer, j, t), :], s_zp_used
                accumulate(zt, w, j, n == 0, n == T2 - 1).then_inc(s_done, 1)

            def layer1(r, j, more):
                fill_after(r, "rep", j, 0, more)
                for t in range(T1):
                    pe.wait_ge(s_z1, product1(r, j, t))
                    rows = rows_of(t)
                    mm = accumulate(z1[0:rows, t, :], w0_sb[0:rows, t, :], j % 2, t == 0, t == T1 - 1)
                    if t == T1 - 1:
                        mm.then_inc(s_layer1, 1)
                    fill_after(r, "shift", j, t, more)
                if j == 2:
                    for n, (kind, _, _) in enumerate(FILLS):
                        if kind == "none":
                            fill(r, n + BC_SLOTS)

            def tower1(part):
                cols = tower_parts[part]
                pe.wait_ge(s_h, 3 * (part + 1))
                for n in range(OUT1 // P):
                    dst = tower1_psum(n)[:, cols]
                    nc.tensor.matmul(dst, wt1a_sb[:, n * P:(n + 1) * P], h_a[:, cols], start=True, stop=False)
                    mm = nc.tensor.matmul(dst, wt1b_sb[:, n * P:(n + 1) * P], h_b[:, cols], start=False,
                                          stop=(part == 0))
                    if part == 0:
                        mm.then_inc(s_m1, 1)

            def tower1_last_pair():
                cols = tower_parts[1]
                pe.wait_ge(s_sum, 6 * NT)
                for n in range(OUT1 // P):
                    nc.tensor.matmul(tower1_psum(n)[:, cols], wt1c_sb[:, n * P:(n + 1) * P], sums[:, 1, 2, cols],
                                     start=False, stop=True).then_inc(s_m1, 1)

            def tower2(part, n):
                cols = tower_parts[part]
                for c in range(OUT1 // P):
                    pe.wait_ge(s_h1, (OUT1 // P) * part + c + 1)
                    mm = nc.tensor.matmul(bc[:, 2, n * B:(n + 1) * B][:, cols], wt2_sb[:, c, n * P:(n + 1) * P],
                                          h1[:, c, cols], start=(c == 0), stop=(c == OUT1 // P - 1))
                mm.then_inc(s_m2, 1)

            def tower3(part):
                cols = tower_parts[part]
                for c in range(OUT2 // P):
                    pe.wait_ge(s_h2, (OUT2 // P) * part + c + 1)
                    mm = nc.tensor.matmul(acc[0:1, 0, cols], wt3_sb[:, c:c + 1], h2[:, c, cols],
                                          start=(c == 0), stop=(c == OUT2 // P - 1))
                mm.then_inc(s_m3, 1)

            def pass_(r, j, more, with_turn, last=False):
                pe.wait_ge(s_relu[1], pair(r, j))
                for n, t in enumerate(ORDER2):
                    layer23(r, "L2", j, t, n)
                    if t in KEPT_TILES and FILLS[FILLS.index(("bc", j, t)) + BC_SLOTS][0] == "bc":
                        fill_after(r, "bc", j, t, more)
                    if n in AHEAD and (more or j == 0):
                        fill(r, FILLS.index(("rep", j + 1, 0)) + AHEAD.index(n))
                    if with_turn and n == TURN_AT:
                        pe.wait_ge(s_relu[3], pair(r, 0))
                        turn(r + 1)
                if j == 0:
                    layer1(r, 1, more)
                elif more:
                    pe.wait_ge(s_all, r + 2)
                    layer1(r, 2, more)
                if last:
                    pe.wait_ge(s_wt, 16 * 9)
                    pe.wait_ge(s_copy, copied(r, "bc", j, KEPT_TILES[-1]))
                    tower1(0)
                pe.wait_ge(s_relu[2], pair(r, j))
                for n, t in enumerate(ORDER3):
                    layer23(r, "L3", j, t, n)
                    if last and n in TOWER2_AT:
                        tower2(0, TOWER2_AT.index(n))
                    if last and n == TOWER3_AT:
                        tower3(0)

            pe.wait_ge(s_const, 16 * 2)
            turn(0)
            pe.wait_ge(s_xp[0], parts(-1, 2))
            for n, (kind, j, t) in enumerate(FILLS):
                if (kind, j) == ("rep", 2) or (kind, j) == ("shift", 2) and t < BC_SLOTS - 1:
                    mm = replicate(n % BC_SLOTS, kind, j, t)
            pe.wait_ge(s_w, 16 * 5)
            pe.wait_ge(s_w0, 3)
            nc.tensor.sem_inc(s_used, DVE_SLOTS)
            nc.tensor.sem_inc(s_zp_used, POOL_SLOTS)
            layer1(-1, 2, True)
            with pe.Fori(0, NT - 1) as r:
                pass_(r, 0, True, False)
                pass_(r, 1, True, True)
            pass_(NT - 1, 0, False, False)
            pass_(NT - 1, 1, False, False, True)
            tower1(1)
            tower1_last_pair()
            for n in range(OUT2 // P):
                tower2(1, n)
            tower3(1)


def selections():
    q = np.arange(P)
    rows = [q % M]
    rows += [(q % M + 4 * t + q // M) % M for t in range(T1)]
    rows += [2 * t + q // H for t in range(T2)]
    return np.concatenate([(np.arange(PARTS * M)[:, None] % M == r[None, :]) for r in rows], axis=1)


def kernel(**inputs):
    import ml_dtypes
    import concourse.bacc as bacc
    from concourse.bass_utils import run_bass_kernel_spmd

    nc = bacc.Bacc("TRN2", target_bir_lowering=False, num_devices=1)
    arrays = {}

    def give(name, a):
        a = np.ascontiguousarray(a)
        arrays[name] = a
        return nc.dram_tensor(name, a.shape, mybir.dt.from_np(a.dtype), kind="ExternalInput").ap()

    w0 = np.asarray(inputs["L0_rec_W0"])
    m = np.arange(M)
    shift = np.arange(M // 2 + 1)[:, None]
    direct = w0[m[None, :], (m[None, :] + shift) % M]
    mirror = w0[(m[None, :] + shift) % M, m[None, :]]
    tiled = [a[:16].reshape(4, P, H).transpose(1, 0, 2) for a in (direct, mirror)]
    last = direct[M // 2, np.arange(P) % M][:, None, :]
    args = [
        give("ids_dram", inputs["ids"]),
        [give(f"tbl_{f}_dram", inputs[f"tbl_{f}"]) for f in range(M)],
        give("sel_dram", selections().astype(ml_dtypes.bfloat16)),
        give("ident_dram", np.eye(P, dtype=np.float32)),
        give("w0a_dram", np.concatenate([tiled[0], last], axis=1)),
        give("w0b_dram", tiled[1]),
        give("w1_dram", inputs["L0_rec_W1"]),
        give("w2_dram", inputs["L0_rec_W2"]),
        give("ctx_dram", np.asarray(inputs["dense_ctx"]).T),
        give("wt1_dram", inputs["W_top1"]),
        give("bt1_dram", np.asarray(inputs["b_top1"]).reshape(OUT1 // P, P).T),
        give("wt2_dram", inputs["W_top2"]),
        give("bt2_dram", np.asarray(inputs["b_top2"]).reshape(OUT2 // P, P).T),
        give("wt3_dram", np.asarray(inputs["W_top3"]).reshape(OUT2 // P, P).T),
    ]
    out = nc.dram_tensor("out_dram", (B, 1), F32, kind="ExternalOutput").ap()
    x_dram = nc.dram_tensor("x_dram", (NT, M, 2 * PAIR), F32).ap()
    interaction_tower(nc, *args, x_dram, out)
    return run_bass_kernel_spmd(nc, [arrays], core_ids=[0]).results[0]["out_dram"]
```

```python
from contextlib import ExitStack

import numpy as np

import concourse.bass as bass
from concourse import mybir

F32 = mybir.dt.float32
BF16 = mybir.dt.bfloat16
I32 = mybir.dt.int32
ALU = mybir.AluOpType
ACT = mybir.ActivationFunctionType
AX_X = mybir.AxisListType.X

B, M, D, H = 512, 32, 16, 64
P = 128
CH = 512
PAIR = 2 * CH
S = PAIR // D
DC = D // 2
NP = B // S
NR = NP // 2
FH = M // 2
OUT1, OUT2, NCTX = 512, 256, 16

T1 = 5
FLAT = T1 - 1
T2 = M * H // P
PARTS = 3

DMA_TILES = (3, 4, 5, 6, 7, 8, 9, 10, 11, 12, 13, 14, 15)
KEPT_TILES = tuple(t for t in range(T2) if t not in DMA_TILES)
ORDER2 = (3, 4, 6, 0, 5, 7, 1, 9, 8, 2, 10, 12, 11, 13, 14, 15)
ORDER3 = DMA_TILES + KEPT_TILES
POOL_TILES = {("L2", 0): (5, 8, 11), ("L3", 0): (5, 8, 11, 14, 0),
              ("L2", 1): (5, 8, 11), ("L3", 1): (5, 8, 11, 14, 0)}
DVE_SLOTS = 6
POOL_SLOTS = 4
BC_SLOTS = 3
GATHERS_FIRST = 11
PAD_AT, TURN_AT, HI_AT, REST_AT, MID_AT, LO_AT, KEEP_AT, REPEAT_AT = 1, 3, 4, 7, 8, 9, 9, 12
PLACE_BEHIND = (9, 10, 11)
WARM_UPS = (16, 9, 12)
WARM_FROM = 7
AHEAD = (12, 13, 14)
TOWER2_AT, TOWER3_AT = (4, 7), 11
ADD_AT = 8
SUM3_AT = 4


def fill_order():
    order = []
    for j in range(2):
        order += [("bc", j, t) for t in ORDER2 if t in KEPT_TILES]
        order += [("shift", j + 1, t) for t in range(FLAT)]
    return order + [("none", 2, 0)] * (-len(order) % BC_SLOTS)


FILLS = fill_order()
REAL_FILLS = [x for x in FILLS if x[0] != "none"]
FIRST_FILLS = FLAT
COPIES = [x for x in FILLS if x[0] == "bc"]
PRODUCTS = [(layer, j, t) for j in range(2) for layer, order in (("L2", ORDER2), ("L3", ORDER3)) for t in order]
DVE_PRODUCTS = [x for x in PRODUCTS if x[2] not in POOL_TILES[x[:2]]]
POOL_PRODUCTS = [x for x in PRODUCTS if x[2] in POOL_TILES[x[:2]]]
assert len(AHEAD) == BC_SLOTS
assert len(DVE_PRODUCTS) % DVE_SLOTS == 0 and len(POOL_PRODUCTS) % POOL_SLOTS == 0
assert all(("L2", j, ORDER2[-1]) in DVE_PRODUCTS and ("L3", j, ORDER3[-1]) in DVE_PRODUCTS for j in range(2))
assert all(x in DVE_PRODUCTS for x in PRODUCTS if x[0] == "L2" and x[2] in KEPT_TILES)


def interaction_tower(nc, ids, starts, table, sel, ident, w0a, w0b, w1, w2, ctx_t,
                      wt1, bt1, wt2, bt2, wt3, x_dram, out):
    with ExitStack() as ctx:
        def sb(name, shape, dt=F32):
            return ctx.enter_context(nc.sbuf_tensor(name, shape, dt))

        def sem(name):
            return ctx.enter_context(nc.semaphore(name))

        idx = sb("idx", [P, FH], I32)
        starts_sb = sb("starts_sb", [P, FH], I32)
        rows = sb("rows", [P, FH], I32)
        emb = sb("emb", [P, 2, FH, D])
        emb_pad = sb("emb_pad", [P, DC, 2 * M])
        unread = sb("unread", [P, 2])
        sel_sb = sb("sel_sb", [PARTS * M, sel.shape[1]], BF16)
        id_sb = sb("id_sb", [P, S])
        x_hi = sb("x_hi", [2 * M, CH], BF16)
        x_mid = sb("x_mid", [2 * M, CH], BF16)
        x_lo = sb("x_lo", [2 * M, CH], BF16)
        x_rest = sb("x_rest", [2 * M, CH])
        xp = sb("xp", [PARTS * M, 2, PAIR], BF16)
        x_rep = sb("x_rep", [P, PAIR])
        first_rest = sb("first_rest", [2 * M, PAIR])
        x_all = sb("x_all", [2 * M, CH])
        x_swap = sb("x_swap", [2 * M, CH])
        x_bc = sb("x_bc", [P, T2, PAIR])
        xk1 = sb("xk1", [P, PAIR])
        xk2 = sb("xk2", [P, PAIR])
        z1 = sb("z1", [P, T1, PAIR])
        z = sb("z", [P, DVE_SLOTS, PAIR])
        zp = sb("zp", [P, POOL_SLOTS, PAIR])
        relu = sb("relu", [P, 2, CH])
        sums = sb("sums", [P, 3, B])
        w0_sb = sb("w0_sb", [P, T1, H])
        w0b_sb = sb("w0b_sb", [P, FLAT, H])
        w1_sb = sb("w1_sb", [P, T2, H])
        w2_sb = sb("w2_sb", [P, T2, H])
        wt1a_sb = sb("wt1a_sb", [P, OUT1])
        wt1b_sb = sb("wt1b_sb", [H + NCTX, OUT1])
        wt1c_sb = sb("wt1c_sb", [P, OUT1])
        wt2_sb = sb("wt2_sb", [P, OUT1 // P, OUT2])
        wt3_sb = sb("wt3_sb", [P, OUT2 // P])
        bt1_sb = sb("bt1_sb", [P, OUT1 // P])
        bt2_sb = sb("bt2_sb", [P, OUT2 // P])
        h_a = sb("h_a", [P, B])
        h_b = sb("h_b", [H + NCTX, B])
        h1 = z1[:, 0:2, :].rearrange("p a (c b) -> p (a c) b", b=B)
        h2 = z1[:, 2, :].rearrange("p (c b) -> p c b", b=B)
        upper = z1[0:H, 3:5, :].rearrange("p a (c b) -> p (a c) b", b=B)[:, 0:3, :]
        y_sb = z1[0:1, 4, B:2 * B]

        acc = ctx.enter_context(nc.psum_tensor("acc", [P, 2, CH], F32))
        bc = ctx.enter_context(nc.psum_tensor("bc", [P, BC_SLOTS, PAIR], F32))

        s_idx = sem("idx_loaded")
        s_zero = sem("padding_zeroed")
        s_rows = sem("rows_numbered")
        s_padded = sem("rows_padded")
        s_go = sem("gathers_may_start")
        s_nearly = sem("all_but_last_of_first_rows_gathered")
        s_gathered = sem("rows_gathered")
        s_const = sem("x_constants_loaded")
        s_w = sem("layer_weights_loaded")
        s_wt = sem("tower_weights_loaded")
        s_w0 = sem("w0_folded")
        s_first_turned = sem("first_pair_turned")
        s_first_hi = sem("first_pair_hi_split")
        s_first_rest = sem("first_pair_rest_left")
        s_first_mid = sem("first_pair_mid_split")
        s_first_lo = sem("first_pair_lo_split")
        s_turned = sem("rows_turned")
        s_hi = sem("hi_split")
        s_rest = sem("rest_left")
        s_mid = sem("mid_split")
        s_lo = sem("lo_split")
        s_xp = [sem(f"parts_in_place_{j}") for j in range(2)]
        s_fill = sem("psum_filled")
        s_copy = sem("replica_copied")
        s_rep_half = sem("half_of_x_rep_written")
        s_rep = sem("x_rep_ready")
        s_all = sem("x_all_ready")
        s_swap = sem("x_swapped")
        s_dram = sem("x_in_dram")
        s_xd = {t: sem(f"replica_{t}_loaded") for t in DMA_TILES}
        s_z1 = sem("layer1_products")
        s_z = sem("products_by_vector")
        s_zp = sem("products_by_gpsimd")
        s_used = sem("vector_products_used")
        s_zp_used = sem("gpsimd_products_used")
        s_layer1 = sem("layer1_accumulated")
        s_xk = {n: sem(f"xk{n}_ready") for n in (1, 2)}
        s_relu = {n: sem(f"relu{n}_ready") for n in (1, 2, 3)}
        s_sum = sem("dims_summed")
        s_upper = sem("upper_moved")
        s_h = sem("tower_input_ready")
        s_m1 = sem("tower1_accumulated")
        s_h1 = sem("tower1_ready")
        s_m2 = sem("tower2_accumulated")
        s_h2 = sem("tower2_ready")
        s_m3 = sem("tower3_accumulated")
        s_y = sem("y_ready")
        s_out = sem("out_written")

        block = ctx.enter_context(nc.Block())

        def filled(r, kind, j, t=0):
            return FIRST_FILLS + r * len(REAL_FILLS) + REAL_FILLS.index((kind, j, t)) + 1

        def gathered(p):
            return 16 * (WARM_FROM + FH * p)

        def relu3_read(r, j):
            return pair(r, j) + 1

        def stored(p):
            return 16 * 2 * (p + 1)

        def swapped(p):
            return 16 * 4 * (p + 1)

        def copied(r, kind, j, t=0):
            return r * len(COPIES) + COPIES.index((kind, j, t)) + 1

        def product(r, layer, j, t):
            return r * len(DVE_PRODUCTS) + DVE_PRODUCTS.index((layer, j, t)) + 1

        def pool_product(r, layer, j, t):
            return r * len(POOL_PRODUCTS) + POOL_PRODUCTS.index((layer, j, t)) + 1

        def product1(r, j, t):
            return T1 * (2 * r + j) + t + 1

        def parts(r):
            return 16 * 2 * PARTS * (r + 1)

        def used(r, layer, j, t):
            return DVE_SLOTS + product(r, layer, j, t)

        def pair(r, j):
            return 2 * r + j + 1

        tower_parts = (slice(0, B - S), slice(B - S, B))

        first_three = bc[0:PARTS * M, FILLS.index(("shift", 2, BC_SLOTS - 1)) % BC_SLOTS, :]
        not_yet_filled = bc[:, FILLS.index(("shift", 2, 0)) % BC_SLOTS, 0:CH]

        def chunk(c):
            return slice(c * CH, (c + 1) * CH)

        def tower1_psum(n):
            return bc[:, n // 2, (n % 2) * B:(n % 2 + 1) * B]

        def fill_slot(kind, j, t=0):
            return FILLS.index((kind, j, t)) % BC_SLOTS

        def product_slot(layer, j, t):
            return DVE_PRODUCTS.index((layer, j, t)) % DVE_SLOTS

        def pool_slot(layer, j, t):
            return POOL_PRODUCTS.index((layer, j, t)) % POOL_SLOTS

        def wait_replica(eng, r, layer, j, t):
            if t in DMA_TILES:
                eng.wait_ge(s_xd[t], 16 * 2 * pair(r, j))
            else:
                eng.wait_ge(s_copy, copied(r, "bc", j, t))

        ids_by_pair = ids.rearrange("(p s) (g f) -> p g s f", s=S, g=2)

        @block.sync
        def _(sp):
            for g in range(2):
                sp.dma_start(idx[g * S:(g + 1) * S, :],
                             ids_by_pair[0, g]).then_inc(s_idx, 16)
            sp.dma_start(starts_sb[:], starts).then_inc(s_idx, 16)

            def place_part(n, j):
                for c in range(2):
                    sp.dma_start(xp[n * M:(n + 1) * M, j, chunk(c)],
                                 (x_hi, x_mid, x_lo)[n][c * M:(c + 1) * M, :]).then_inc(s_xp[j], 16)

            sp.dma_start(sel_sb[:], sel).then_inc(s_const, 16)
            for g in range(2):
                sp.dma_start(id_sb[g * S:(g + 1) * S, :], ident).then_inc(s_const, 16)
            sp.dma_start(w0_sb[:], w0a).then_inc(s_w, 16)
            sp.dma_start(w0b_sb[:], w0b).then_inc(s_w, 16)
            sp.dma_start(w1_sb[:], w1.rearrange("m h k -> (m h) k").rearrange("(t p) k -> p t k", p=P)
                         ).then_inc(s_w, 16)
            sp.dma_start(w2_sb[:], w2.rearrange("m h k -> (m h) k").rearrange("(t p) k -> p t k", p=P)
                         ).then_inc(s_w, 16)
            sp.dma_start(wt1a_sb[:], wt1[0:P, :]).then_inc(s_wt, 16)
            sp.dma_start(wt1b_sb[:], wt1[P:P + H + NCTX, :]).then_inc(s_wt, 16)
            for q in range(2):
                sp.dma_start(wt1c_sb[q * H:(q + 1) * H, :], wt1[P:P + H, :]).then_inc(s_wt, 16)
            sp.dma_start(wt2_sb[:], wt2.rearrange("(t p) n -> p t n", p=P)).then_inc(s_wt, 16)
            sp.dma_start(wt3_sb[:], wt3).then_inc(s_wt, 16)
            sp.dma_start(bt1_sb[:], bt1).then_inc(s_wt, 16)
            sp.dma_start(bt2_sb[:], bt2).then_inc(s_wt, 16)
            sp.dma_start(h_b[H:H + NCTX, :], ctx_t).then_inc(s_wt, 16)

            def store_x(p):
                sp.wait_ge(s_all, p + 1)
                for c in range(2):
                    sp.dma_start(x_dram[p, :, chunk(c)], x_all[c * M:(c + 1) * M, :]).then_inc(s_dram, 16)

            def swap_halves():
                for q in range(0, 2 * M, M):
                    for to, of in ((q, q + M // 2), (q + M // 2, q)):
                        sp.dma_start(x_swap[to:to + M // 2, :], x_all[of:of + M // 2, :]).then_inc(s_swap, 16)

            def load_replicas(p, t):
                for q in range(2):
                    row = x_dram[p, 2 * t + q:2 * t + q + 1, :]
                    sp.dma_start(x_bc[q * H:(q + 1) * H, t, :], row.to_broadcast([H, PAIR])
                                 ).then_inc(s_xd[t], 16)

            sp.wait_ge(s_rows, 1)
            for g in range(2):
                sp.dma_start(idx[g * S:(g + 1) * S, :], ids_by_pair[1, g]).then_inc(s_idx, 16)
            store_x(0)
            swap_halves()
            sp.wait_ge(s_dram, stored(0))
            for n, t in enumerate(DMA_TILES):
                load_replicas(0, t)
                if n in PLACE_BEHIND:
                    part = PLACE_BEHIND.index(n)
                    sp.wait_ge((s_hi, s_mid, s_lo)[part], 1)
                    place_part(part, 1)

            def pass_(r, j, more):
                p = 2 * r + j
                store_x(p + 1)
                sp.wait_ge(s_dram, stored(p + 1))
                swap_halves()
                for t in DMA_TILES:
                    if ("L3", j, t) in DVE_PRODUCTS:
                        sp.wait_ge(s_z, product(r, "L3", j, t))
                    else:
                        sp.wait_ge(s_zp, pool_product(r, "L3", j, t))
                    load_replicas(p + 1, t)
                if more:
                    for n, s_part in enumerate((s_hi, s_mid, s_lo)):
                        sp.wait_ge(s_part, p + 2)
                        place_part(n, j)

            with sp.Fori(0, NR - 1) as r:
                for j in range(2):
                    pass_(r, j, True)
            pass_(NR - 1, 0, False)

            sp.wait_ge(s_y, 2)
            sp.dma_start(out.rearrange("b n -> n b"), y_sb).then_inc(s_out, 16)
            sp.wait_ge(s_out, 16)

        @block.gpsimd
        def _(pool):
            def number_rows(p):
                pool.wait_ge(s_idx, 16 * (2 * p + 3))
                nc.gpsimd.tensor_tensor(rows[:], idx[:], starts_sb[:], ALU.add).then_inc(s_rows, 1)

            def gather(j, first, last, s_done=s_gathered):
                for f in range(first, last):
                    nc.gpsimd.indirect_dma_start(
                        emb[:, j, f, :], None, table,
                        bass.IndirectOffsetOnAxis(rows[:, f:f + 1], axis=0)).then_inc(s_done, 16)

            def multiply(r, layer, j):
                xk, s_ready = (xk1, s_xk[1]) if layer == "L2" else (xk2, s_xk[2])
                pool.wait_ge(s_ready, 4 * pair(r, j))
                for which, _, t in [x for x in POOL_PRODUCTS if x[:2] == (layer, j)]:
                    wait_replica(pool, r, layer, j, t)
                    pool.wait_ge(s_zp_used, pool_product(r, layer, j, t))
                    nc.gpsimd.tensor_tensor(zp[:, pool_slot(layer, j, t), :], x_bc[:, t, :], xk[:],
                                            ALU.mult).then_inc(s_zp, 1)

            def pass_(r, j, more):
                multiply(r, "L2", j)
                if more:
                    p = 2 * r + j + 2
                    pool.wait_ge(s_gathered, gathered(p - 1))
                    number_rows(p)
                    pool.wait_ge(s_padded, 2 * (p - 1))
                    pool.wait_ge(s_rows, p + 1)
                    nc.gpsimd.sem_inc(s_go, 1)
                    gather(j, 0, GATHERS_FIRST)
                multiply(r, "L3", j)
                if more:
                    gather(j, GATHERS_FIRST, FH)

            number_rows(0)
            pool.wait_ge(s_rows, 1)
            gather(0, 0, FH - WARM_FROM, s_nearly)
            gather(0, FH - WARM_FROM, FH)
            pool.wait_ge(s_gathered, gathered(0))
            pool.wait_ge(s_nearly, 16 * (FH - WARM_FROM))
            number_rows(1)
            pool.wait_ge(s_rows, 2)
            gather(1, 0, FH)
            with pool.Fori(0, NR - 1) as r:
                for j in range(2):
                    pass_(r, j, True)
            for j in range(2):
                pass_(NR - 1, j, False)

        @block.scalar
        def _(act):
            def copy_bc(r, j, t):
                act.wait_ge(s_z, product(r, "L2", j, t))
                nc.scalar.activation(x_bc[:, t, :], bc[:, fill_slot("bc", j, t), :], ACT.Copy).then_inc(s_copy, 1)

            def repeat_x(n, p):
                act.wait_ge(s_all, p + 1)
                for c in range(2):
                    for q in range(2):
                        nc.scalar.activation(x_rep[q * M:(q + 1) * M, chunk(c)], x_all[c * M:(c + 1) * M, :],
                                             ACT.Copy).then_inc(s_rep_half, 1)
                act.wait_ge(s_rep_half, 4 * n)
                nc.scalar.activation(x_rep[2 * M:, :], x_rep[0:2 * M, :], ACT.Copy).then_inc(s_rep, 1)

            def pad(j):
                padded = emb_pad[:].rearrange("p d (c g f) -> p g d c f", c=2, g=2)
                for g in range(2):
                    nc.scalar.activation(padded[g * S:(g + 1) * S, g, :, :, :],
                                         emb[g * S:(g + 1) * S, j, :, :].rearrange("p f (c d) -> p d c f", c=2),
                                         ACT.Copy).then_inc(s_padded, 1)

            def split_hi(n, at):
                act.wait_ge(s_turned, n)
                nc.scalar.activation(x_hi[:], acc[0:2 * M, at, :], ACT.Copy).then_inc(s_hi, 1)

            def keep_x(at):
                nc.scalar.activation(x_all[:], acc[0:2 * M, at, :], ACT.Copy).then_inc(s_all, 1)

            def split_mid(n):
                act.wait_ge(s_rest, n)
                nc.scalar.activation(x_mid[:], x_rest[:], ACT.Copy).then_inc(s_mid, 1)

            def evacuate(layer, at):
                if layer < 3:
                    xk = (xk1, xk2)[layer - 1]
                    for c in range(2):
                        for half in range(2):
                            nc.scalar.activation(xk[half * H:(half + 1) * H, c * CH:(c + 1) * CH],
                                                 acc[c * H:(c + 1) * H, at, :], ACT.Relu).then_inc(s_xk[layer], 1)
                nc.scalar.activation(relu[:, at, :], acc[:, at, :], ACT.Relu).then_inc(s_relu[layer], 1)

            def move_upper(part):
                act.wait_ge(s_sum, 3 * NP - 2 + part)
                cols, layers = tower_parts[part], slice(0, 3 - part)
                nc.scalar.activation(upper[:, layers, cols], sums[H:P, layers, cols], ACT.Copy).then_inc(s_upper, 1)

            def tower1(part):
                cols = tower_parts[part]
                for n in range(OUT1 // P):
                    act.wait_ge(s_m1, (OUT1 // P) * part + n + 1)
                    nc.scalar.activation(h1[:, n, cols], tower1_psum(n)[:, cols], ACT.Relu,
                                         bias=bt1_sb[:, n:n + 1]).then_inc(s_h1, 1)

            def tower2_and_3(part):
                cols = tower_parts[part]
                for n in range(OUT2 // P):
                    act.wait_ge(s_m2, (OUT2 // P) * part + n + 1)
                    nc.scalar.activation(h2[:, n, cols], bc[:, 2, n * B:(n + 1) * B][:, cols], ACT.Relu,
                                         bias=bt2_sb[:, n:n + 1]).then_inc(s_h2, 1)
                act.wait_ge(s_m3, part + 1)
                nc.scalar.activation(y_sb[:, cols], acc[0:1, 0, cols], ACT.Copy).then_inc(s_y, 1)

            def pass_(r, j, more, last=False, load=False):
                if load:
                    act.wait_ge(s_rows, 2 * r + j + 2)
                    for g in range(2):
                        act.dma_start(idx[g * S:(g + 1) * S, :], ids_by_pair[2 * r + j + 2, g]).then_inc(s_idx, 16)
                for n, t in enumerate(ORDER2):
                    if t in KEPT_TILES:
                        copy_bc(r, j, t)
                    if last and n == 7:
                        move_upper(0)
                    if more and n == PAD_AT:
                        act.wait_ge(s_gathered, gathered(2 * r + j + 1))
                        pad(1 - j)
                    if more and n == HI_AT:
                        split_hi(pair(r, j), 1 - j)
                    if more and n == MID_AT:
                        split_mid(pair(r, j))
                    if more and n == KEEP_AT:
                        act.wait_ge(s_rest, pair(r, j))
                        act.wait_ge(s_dram, stored(2 * r + j))
                        act.wait_ge(s_swap, swapped(2 * r + j))
                        keep_x(1 - j)
                    if more and n == REPEAT_AT:
                        repeat_x(pair(r, j), 2 * r + j + 1)
                act.wait_ge(s_used, used(r, "L2", j, ORDER2[-1]))
                evacuate(2, j)
                if more:
                    act.wait_ge(s_layer1, 2 * pair(r, j + 1))
                    evacuate(1, 1 - j)
                if last:
                    act.wait_ge(s_wt, 16 * 9)
                    tower1(0)
                    move_upper(1)
                    tower2_and_3(0)
                act.wait_ge(s_used, used(r, "L3", j, ORDER3[-1]))
                evacuate(3, j)

            nc.scalar.sem_inc(s_relu[3], 1)
            act.wait_ge(s_zero, 1)
            nc.scalar.activation(unread[:, 1:2], unread[:, 0:1], ACT.Copy)
            act.wait_ge(s_nearly, 16 * (FH - WARM_FROM))
            act.wait_ge(s_gathered, gathered(0))
            pad(0)
            for c in range(2):
                act.wait_ge(s_first_turned, c + 1)
                nc.scalar.activation(xp[0:PARTS * M, 0, chunk(c)], first_three[:, chunk(c)], ACT.Copy
                                     ).then_inc(s_first_hi, 1)
            for c in range(2):
                act.wait_ge(s_first_rest, c + 1)
                nc.scalar.activation(xp[0:2 * M, 0, chunk(c)], first_rest[:, chunk(c)], ACT.Copy
                                     ).then_inc(s_first_mid, 1)
            nc.scalar.activation(x_rep[0:PARTS * M, :], first_three, ACT.Copy)
            nc.scalar.activation(x_rep[PARTS * M:, :], first_three[0:M, :], ACT.Copy).then_inc(s_rep, 1)
            for c in range(2):
                kept = nc.scalar.activation(x_all[c * M:(c + 1) * M, :], first_three[0:M, chunk(c)], ACT.Copy)
            kept.then_inc(s_all, 1)
            act.wait_ge(s_layer1, 2)
            evacuate(1, 0)
            with act.Fori(0, NR - 1) as r:
                for j in range(2):
                    pass_(r, j, True, load=True)
            pass_(NR - 1, 0, True)
            pass_(NR - 1, 1, False, True)
            tower1(1)
            tower2_and_3(1)

        @block.vector
        def _(dve):
            def subtract_hi(n, at):
                dve.wait_ge(s_hi, n)
                nc.vector.tensor_tensor(x_rest[:], acc[0:2 * M, at, :], x_hi[:], ALU.subtract).then_inc(s_rest, 1)

            def split_lo(n):
                dve.wait_ge(s_mid, n)
                nc.vector.tensor_tensor(x_lo[:], x_rest[:], x_mid[:], ALU.subtract).then_inc(s_lo, 1)

            def sum_dims(layer, n, j, p):
                dve.wait_ge(s_relu[layer], n)
                nc.vector.tensor_reduce(sums[:, layer - 1, bass.ts(p, S)],
                                        relu[:, j, :].rearrange("p (d b) -> p b d", b=S),
                                        AX_X, ALU.add).then_inc(s_sum, 1)

            def multiply1(r, j):
                dve.wait_ge(s_rep, 2 * r + j + 1)
                for t in range(FLAT):
                    dve.wait_ge(s_fill, filled(r, "shift", j, t))
                    nc.vector.tensor_tensor(z1[:, t, :], bc[:, fill_slot("shift", j, t), :], x_rep[:],
                                            ALU.mult).then_inc(s_z1, 1)
                dve.wait_ge(s_all, 2 * r + j + 1)
                dve.wait_ge(s_swap, swapped(2 * r + j))
                nc.vector.tensor_tensor(z1[0:2 * M, FLAT, 0:CH], x_all[:], x_swap[:], ALU.mult).then_inc(s_z1, 1)

            def multiply(r, layer, j, t):
                dve.wait_ge(s_used, product(r, layer, j, t))
                out_z = z[:, product_slot(layer, j, t), :]
                if layer == "L2" and t in KEPT_TILES:
                    dve.wait_ge(s_fill, filled(r, "bc", j, t))
                    x = bc[:, fill_slot("bc", j, t), :]
                else:
                    wait_replica(dve, r, layer, j, t)
                    x = x_bc[:, t, :]
                nc.vector.tensor_tensor(out_z, x, (xk1 if layer == "L2" else xk2)[:], ALU.mult).then_inc(s_z, 1)

            def add_chunks(part):
                dve.wait_ge(s_upper, part + 1)
                dve.wait_ge(s_sum, 3 * NP - 2 + part)
                cols = tower_parts[part]
                for n, dst in list(enumerate((h_a[0:H, cols], h_a[H:P, cols], h_b[0:H, cols])))[:3 - part]:
                    nc.vector.tensor_tensor(dst, sums[0:H, n, cols], upper[:, n, cols], ALU.add).then_inc(s_h, 1)

            def layer2(r, j, steps, turn=False):
                if 0 in steps:
                    dve.wait_ge(s_xk[1], 4 * pair(r, j))
                for n in steps:
                    if ("L2", j, ORDER2[n]) in DVE_PRODUCTS:
                        multiply(r, "L2", j, ORDER2[n])
                    if turn and n == REST_AT:
                        subtract_hi(pair(r, j), 1 - j)
                    if turn and n == LO_AT:
                        split_lo(pair(r, j))

            def layers1_and_3(r, j, more):
                if more:
                    multiply1(r, j + 1)
                dve.wait_ge(s_xk[2], 4 * pair(r, j))
                for n, t in enumerate(ORDER3):
                    if ("L3", j, t) in DVE_PRODUCTS:
                        multiply(r, "L3", j, t)
                    if n == 1:
                        sum_dims(2, pair(r, j), j, 2 * r + j)
                    if more and n == 4:
                        sum_dims(1, pair(r, j + 1), 1 - j, 2 * r + j + 1)
                    if not more and n == ADD_AT:
                        add_chunks(1)

            def round_(r, more):
                layer2(r, 0, range(SUM3_AT + 1, T2), True)
                layers1_and_3(r, 0, True)
                layer2(r, 1, range(SUM3_AT + 1))
                sum_dims(3, relu3_read(r, 0), 0, 2 * r)
                layer2(r, 1, range(SUM3_AT + 1, T2), more)
                if not more:
                    add_chunks(0)
                layers1_and_3(r, 1, more)
                if more:
                    layer2(r + 1, 0, range(SUM3_AT + 1))
                sum_dims(3, relu3_read(r, 1), 1, 2 * r + 1)

            nc.vector.memset(unread[:], 0.0)
            nc.vector.memset(emb_pad[:], 0.0).then_inc(s_zero, 1)
            dve.wait_ge(s_w, 16 * 4)
            for q, rows, t in ((M, M, 0), (2 * M, 2 * M, 0), (0, M, 1)):
                w, wb = w0_sb[q:q + rows, t:FLAT, :], w0b_sb[q:q + rows, t:, :]
                nc.vector.tensor_tensor(w, w, wb, ALU.add).then_inc(s_w0, 1)
            for c in range(2):
                dve.wait_ge(s_first_hi, c + 1)
                nc.vector.tensor_tensor(first_rest[:, chunk(c)], first_three[0:2 * M, chunk(c)],
                                        xp[0:2 * M, 0, chunk(c)], ALU.subtract).then_inc(s_first_rest, 1)
            for c in range(2):
                dve.wait_ge(s_first_mid, c + 1)
                nc.vector.tensor_tensor(xp[0:M, 0, chunk(c)], first_rest[0:M, chunk(c)],
                                        xp[0:M, 0, chunk(c)], ALU.subtract).then_inc(s_first_lo, 1)
            multiply1(-1, 2)
            layer2(0, 0, range(SUM3_AT + 1))
            sum_dims(1, 1, 0, 0)
            with dve.Fori(0, NR - 1) as r:
                round_(r, True)
            round_(NR - 1, False)

        @block.tensor
        def _(pe):
            def keep_warm(times, unused):
                for _ in range(times):
                    nc.tensor.matmul(unused, sel_sb[:, 0:P], sel_sb[:, 0:CH], start=True, stop=True)

            def turn_first_pair():
                pe.wait_ge(s_padded, 2)
                for c in range(2):
                    for dd, part in np.ndindex(DC, PARTS):
                        q = c * DC + dd
                        mm = nc.tensor.matmul(first_three[part * M:(part + 1) * M, q * S:(q + 1) * S],
                                              emb_pad[:, dd, c * M:(c + 1) * M], id_sb[:], start=True, stop=True)
                    mm.then_inc(s_first_turned, 1)

            def turn(p, at):
                pe.wait_ge(s_padded, 2 * (p + 1))
                for dd in range(DC):
                    mm = nc.tensor.matmul(acc[0:2 * M, at, dd * S:(dd + 1) * S], emb_pad[:, dd, :],
                                          id_sb[:], start=True, stop=True)
                mm.then_inc(s_turned, 1)

            def replicate(slot, kind, j, t):
                n = {"shift": t, "bc": FLAT + t}[kind]
                for c in range(2):
                    mm = nc.tensor.matmul(bc[:, slot, c * CH:(c + 1) * CH], sel_sb[:, n * P:(n + 1) * P],
                                          xp[:, j % 2, c * CH:(c + 1) * CH], start=True, stop=True)
                mm.then_inc(s_fill, 1)

            def fill(r, n):
                before, r_before = n - BC_SLOTS, r
                if FILLS[before][0] == "none":
                    before -= BC_SLOTS
                if before < 0:
                    before, r_before = before + len(FILLS), r - 1
                kind, j, t = FILLS[before]
                if kind == "shift":
                    pe.wait_ge(s_z1, product1(r_before, j, t))
                else:
                    pe.wait_ge(s_copy, copied(r_before, kind, j, t))
                kind, j, t = FILLS[n % len(FILLS)]
                if (kind, t) == ("shift", 0):
                    pe.wait_ge(s_xp[j % 2], parts(r))
                replicate(n % BC_SLOTS, kind, j, t)

            def fill_after(r, kind, j, t, more):
                n = FILLS.index((kind, j, t)) + BC_SLOTS
                next_kind, next_j, _ = FILLS[n % len(FILLS)]
                if next_kind == "bc" or next_kind == "shift" and kind != "bc" and next_j == j:
                    if more or n < FILLS.index(("shift", 2, 0)):
                        fill(r, n)

            def accumulate(zt, w, at, first, last):
                for c in range(2):
                    mm = nc.tensor.matmul(acc[c * H:(c + 1) * H, at, :], w, zt[:, chunk(c)],
                                          start=first, stop=last)
                return mm

            def accumulate_flat(j):
                for c in range(2):
                    rows = slice(c * M, (c + 1) * M)
                    nc.tensor.matmul(acc[c * H:(c + 1) * H, j % 2, :], w0_sb[rows, FLAT, :],
                                     z1[rows, FLAT, 0:CH], start=False, stop=True).then_inc(s_layer1, 1)

            def layer23(r, layer, j, t, n):
                w = (w1_sb if layer == "L2" else w2_sb)[:, t, :]
                if (layer, j, t) in DVE_PRODUCTS:
                    pe.wait_ge(s_z, product(r, layer, j, t))
                    zt, s_done = z[:, product_slot(layer, j, t), :], s_used
                else:
                    pe.wait_ge(s_zp, pool_product(r, layer, j, t))
                    zt, s_done = zp[:, pool_slot(layer, j, t), :], s_zp_used
                accumulate(zt, w, j, n == 0, n == T2 - 1).then_inc(s_done, 1)

            def layer1(r, j, more):
                for t in range(FLAT):
                    pe.wait_ge(s_z1, product1(r, j, t))
                    accumulate(z1[:, t, :], w0_sb[:, t, :], j % 2, t == 0, False)
                    fill_after(r, "shift", j, t, more)
                pe.wait_ge(s_z1, product1(r, j, FLAT))
                accumulate_flat(j)
                if j == 2:
                    for n, (kind, _, _) in enumerate(FILLS):
                        if kind == "none" and FILLS[(n + BC_SLOTS) % len(FILLS)][0] == "bc":
                            fill(r, n + BC_SLOTS)

            def tower1(part):
                cols = tower_parts[part]
                below = slice(H if part else 0, H + NCTX)
                pe.wait_ge(s_h, 3 + 2 * part)
                for n in range(OUT1 // P):
                    dst = tower1_psum(n)[:, cols]
                    nc.tensor.matmul(dst, wt1a_sb[:, n * P:(n + 1) * P], h_a[:, cols], start=True, stop=False)
                    mm = nc.tensor.matmul(dst, wt1b_sb[below, n * P:(n + 1) * P], h_b[below, cols], start=False,
                                          stop=(part == 0))
                    if part == 0:
                        mm.then_inc(s_m1, 1)

            def tower1_last_pair():
                cols = tower_parts[1]
                pe.wait_ge(s_sum, 3 * NP)
                for n in range(OUT1 // P):
                    nc.tensor.matmul(tower1_psum(n)[:, cols], wt1c_sb[:, n * P:(n + 1) * P], sums[:, 2, cols],
                                     start=False, stop=True).then_inc(s_m1, 1)

            def tower2(part, n):
                cols = tower_parts[part]
                for c in range(OUT1 // P):
                    pe.wait_ge(s_h1, (OUT1 // P) * part + c + 1)
                    mm = nc.tensor.matmul(bc[:, 2, n * B:(n + 1) * B][:, cols], wt2_sb[:, c, n * P:(n + 1) * P],
                                          h1[:, c, cols], start=(c == 0), stop=(c == OUT1 // P - 1))
                mm.then_inc(s_m2, 1)

            def tower3(part):
                cols = tower_parts[part]
                for c in range(OUT2 // P):
                    pe.wait_ge(s_h2, (OUT2 // P) * part + c + 1)
                    mm = nc.tensor.matmul(acc[0:1, 0, cols], wt3_sb[:, c:c + 1], h2[:, c, cols],
                                          start=(c == 0), stop=(c == OUT2 // P - 1))
                mm.then_inc(s_m3, 1)

            def pass_(r, j, more, last=False):
                pe.wait_ge(s_relu[1], pair(r, j))
                for n, t in enumerate(ORDER2):
                    layer23(r, "L2", j, t, n)
                    if t in KEPT_TILES:
                        fill_after(r, "bc", j, t, more)
                    if n in AHEAD and (more or j == 0):
                        fill(r, FILLS.index(("shift", j + 1, 0)) + AHEAD.index(n))
                    if not last and n == TURN_AT:
                        pe.wait_ge(s_relu[3], relu3_read(r, j - 1))
                        turn(2 * r + j + 1, 1 - j)
                if not last:
                    pe.wait_ge(s_all, 2 * r + j + 2)
                    layer1(r, j + 1, more)
                if last:
                    pe.wait_ge(s_wt, 16 * 9)
                    pe.wait_ge(s_copy, copied(r, "bc", j, KEPT_TILES[-1]))
                    tower1(0)
                pe.wait_ge(s_relu[2], pair(r, j))
                for n, t in enumerate(ORDER3):
                    layer23(r, "L3", j, t, n)
                    if last and n in TOWER2_AT:
                        tower2(0, TOWER2_AT.index(n))
                    if last and n == TOWER3_AT:
                        tower3(0)

            pe.wait_ge(s_const, 16 * 3)
            pe.wait_ge(s_nearly, 16 * (FH - WARM_FROM))
            keep_warm(WARM_UPS[0], not_yet_filled)
            turn_first_pair()
            keep_warm(WARM_UPS[1], not_yet_filled)
            pe.wait_ge(s_first_lo, 2)
            for n, (kind, j, t) in enumerate(FILLS):
                if (kind, j) == ("shift", 2) and t < BC_SLOTS:
                    if t == BC_SLOTS - 1:
                        pe.wait_ge(s_all, 1)
                    replicate(n % BC_SLOTS, kind, j, t)
            pe.wait_ge(s_w, 16 * 4)
            pe.wait_ge(s_w0, 3)
            nc.tensor.sem_inc(s_used, DVE_SLOTS)
            nc.tensor.sem_inc(s_zp_used, POOL_SLOTS)
            layer1(-1, 2, True)
            keep_warm(WARM_UPS[2], acc[:, 1, :])
            with pe.Fori(0, NR - 1) as r:
                for j in range(2):
                    pass_(r, j, True)
            pass_(NR - 1, 0, False)
            pass_(NR - 1, 1, False, True)
            tower1(1)
            tower1_last_pair()
            for n in range(OUT2 // P):
                tower2(1, n)
            tower3(1)


def selections():
    q = np.arange(P)
    rows = [(q % M + 4 * t + q // M) % M for t in range(FLAT)]
    rows += [2 * t + q // H for t in range(T2)]
    return np.concatenate([(np.arange(PARTS * M)[:, None] % M == r[None, :]) for r in rows], axis=1)


def kernel(**inputs):
    import ml_dtypes
    import concourse.bacc as bacc
    from concourse.bass_utils import run_bass_kernel_spmd

    nc = bacc.Bacc("TRN2", target_bir_lowering=False, num_devices=1)
    arrays = {}

    def give(name, a):
        a = np.ascontiguousarray(a)
        arrays[name] = a
        return nc.dram_tensor(name, a.shape, mybir.dt.from_np(a.dtype), kind="ExternalInput").ap()

    w0 = np.asarray(inputs["L0_rec_W0"])
    m = np.arange(M)
    shift = np.arange(M // 2 + 1)[:, None]
    direct = w0[m[None, :], (m[None, :] + shift) % M]
    mirror = w0[(m[None, :] + shift) % M, m[None, :]]
    tiled = [a[:16].reshape(4, P, H).transpose(1, 0, 2) for a in (direct, mirror)]
    last = direct[M // 2, np.arange(P) % M][:, None, :]
    starts = np.cumsum([0] + [inputs[f"tbl_{f}"].shape[0] for f in range(M - 1)]).astype(np.int32)
    args = [
        give("ids_dram", inputs["ids"]),
        give("starts_dram", np.repeat(starts.reshape(2, FH), S, axis=0)),
        give("table_dram", np.concatenate([inputs[f"tbl_{f}"] for f in range(M)], axis=0)),
        give("sel_dram", selections().astype(ml_dtypes.bfloat16)),
        give("ident_dram", np.eye(S, dtype=np.float32)),
        give("w0a_dram", np.concatenate([tiled[0], last], axis=1)),
        give("w0b_dram", tiled[1]),
        give("w1_dram", inputs["L0_rec_W1"]),
        give("w2_dram", inputs["L0_rec_W2"]),
        give("ctx_dram", np.asarray(inputs["dense_ctx"]).T),
        give("wt1_dram", inputs["W_top1"]),
        give("bt1_dram", np.asarray(inputs["b_top1"]).reshape(OUT1 // P, P).T),
        give("wt2_dram", inputs["W_top2"]),
        give("bt2_dram", np.asarray(inputs["b_top2"]).reshape(OUT2 // P, P).T),
        give("wt3_dram", np.asarray(inputs["W_top3"]).reshape(OUT2 // P, P).T),
    ]
    out = nc.dram_tensor("out_dram", (B, 1), F32, kind="ExternalOutput").ap()
    x_dram = nc.dram_tensor("x_dram", (NP, M, PAIR), F32).ap()
    interaction_tower(nc, *args, x_dram, out)
    return run_bass_kernel_spmd(nc, [arrays], core_ids=[0]).results[0]["out_dram"]
```
